# Optimizing a Trainium2 kernel written in Bass

```python
import numpy as np
import jax
import jax.numpy as jnp

def _softmax(x, axis=-1):
    return jax.nn.softmax(x, axis=axis)

def _gelu(x):
    return jax.nn.gelu(x, approximate=True)

def _silu(x):
    return jax.nn.silu(x)

def _sigmoid(x):
    return jax.nn.sigmoid(x)

def _layernorm(x, axis=-1, eps=1e-05):
    m = jnp.mean(x, axis=axis, keepdims=True)
    v = jnp.var(x, axis=axis, keepdims=True)
    return (x - m) / jnp.sqrt(v + eps)

def _scatter_add(tgt, idx, src, axis=0):
    return tgt.at[idx].add(src)

def _segment_sum(src, seg, n):
    return jax.ops.segment_sum(src, seg, n)
kernel_name = 'mk_conv_seq_d2_conv_nchw384_r4_2826e3'

def setup_inputs(seed: int=0):
    np.random.seed(seed)
    _w = jnp.asarray

    def _rec_inputs():
        import jax
        import jax.numpy as jnp
        _gk = jax.random.key(seed)
        x = -0.000357 + 1 * jax.random.normal(jax.random.fold_in(_gk, 1), (16, 96, 56, 56), jnp.float32)
        return x
    x = _rec_inputs()

    def _L0_conv_setup():
        import jax, jax.numpy as jnp
        import numpy as np
        DIM = 96
        HID = 4 * DIM
        EPS = 1e-06
        GRN_EPS = 1e-06

        def _block(x, dw_w, dw_b, ln_w, ln_b, w1, b1, grn_gamma, grn_beta, w2, b2):
            identity = x
            y = jax.lax.conv_general_dilated(x, dw_w, window_strides=(1, 1), padding=((3, 3), (3, 3)), dimension_numbers=('NCHW', 'OIHW', 'NCHW'), feature_group_count=DIM)
            y = y + dw_b[None, :, None, None]
            y = jnp.transpose(y, (0, 2, 3, 1))
            mu = jnp.mean(y, axis=-1, keepdims=True)
            var = jnp.mean(jnp.square(y - mu), axis=-1, keepdims=True)
            y = (y - mu) * jax.lax.rsqrt(var + EPS) * ln_w + ln_b
            y = jnp.einsum('bhwc,cd->bhwd', y, w1) + b1
            y = jax.nn.gelu(y, approximate=False)
            gx = jnp.sqrt(jnp.sum(jnp.square(y), axis=(1, 2), keepdims=True))
            nx = gx / (jnp.mean(gx, axis=-1, keepdims=True) + GRN_EPS)
            y = grn_gamma * (y * nx) + grn_beta + y
            y = jnp.einsum('bhwd,dc->bhwc', y, w2) + b2
            return identity + jnp.transpose(y, (0, 3, 1, 2))
        key = jax.random.key(seed)
        ks = jax.random.split(key, 8)
        x = jax.random.normal(ks[0], (16, DIM, 56, 56), dtype=jnp.float32)
        dw_w = jax.random.normal(ks[1], (DIM, 1, 7, 7), dtype=jnp.float32) * 0.02
        dw_b = jnp.zeros((DIM,), dtype=jnp.float32)
        ln_w = jnp.ones((DIM,), dtype=jnp.float32)
        ln_b = jnp.zeros((DIM,), dtype=jnp.float32)
        w1 = jax.random.normal(ks[2], (DIM, HID), dtype=jnp.float32) * 0.02
        b1 = jnp.zeros((HID,), dtype=jnp.float32)
        grn_gamma = jnp.zeros((HID,), dtype=jnp.float32)
        grn_beta = jnp.zeros((HID,), dtype=jnp.float32)
        w2 = jax.random.normal(ks[3], (HID, DIM), dtype=jnp.float32) * 0.02
        b2 = jnp.zeros((DIM,), dtype=jnp.float32)
        return {'x': x, 'dw_w': dw_w, 'dw_b': dw_b, 'ln_w': ln_w, 'ln_b': ln_b, 'w1': w1, 'b1': b1, 'grn_gamma': grn_gamma, 'grn_beta': grn_beta, 'w2': w2, 'b2': b2}
    _L0_conv_all = _L0_conv_setup()
    _L0_conv_in = {k: v for k, v in _L0_conv_all.items() if k in ('dw_w', 'dw_b', 'ln_w', 'ln_b', 'w1', 'b1', 'grn_gamma', 'grn_beta', 'w2', 'b2')}
    del _L0_conv_all

    def _L1_conv_setup():
        import jax, jax.numpy as jnp
        import numpy as np
        DIM = 96
        FRACTION = 16
        INTEGER = 16
        WEIGHT_BITS = 5
        SHIFT_MIN = -(2 ** (WEIGHT_BITS - 1) - 2)

        def _ste(x, qx):
            return x + jax.lax.stop_gradient(qx - x)

        def _clampabs(w, mn, mx):
            return jnp.sign(w) * jnp.clip(jnp.abs(w), mn, mx)

        def _round_power_of_2(w):
            shift = jnp.round(jnp.log2(jnp.maximum(jnp.abs(w), 1e-30)))
            return jnp.sign(w) * jnp.exp2(shift)

        def _round_to_fixed(x, fraction=FRACTION, integer=INTEGER):
            delta = 2.0 ** (-fraction)
            bound = 2.0 ** (integer - 1)
            return jnp.clip(jnp.floor(x / delta) * delta, -bound, bound - 1)
        key = jax.random.key(seed)
        k1, k2, k3 = jax.random.split(key, 3)
        x = jax.random.normal(k1, (32, DIM, 56, 56), dtype=jnp.float32)
        weight = jax.random.normal(k2, (DIM, 1, 3, 3), dtype=jnp.float32) * 0.1
        bias = jax.random.normal(k3, (DIM,), dtype=jnp.float32) * 0.01
        return {'x': x, 'weight': weight, 'bias': bias}
    _L1_conv_all = _L1_conv_setup()
    _L1_conv_in = {k: v for k, v in _L1_conv_all.items() if k in ('weight', 'bias')}
    del _L1_conv_all
    return {'x': x, 'L0_conv_dw_w': _L0_conv_in['dw_w'], 'L0_conv_dw_b': _L0_conv_in['dw_b'], 'L0_conv_ln_w': _L0_conv_in['ln_w'], 'L0_conv_ln_b': _L0_conv_in['ln_b'], 'L0_conv_w1': _L0_conv_in['w1'], 'L0_conv_b1': _L0_conv_in['b1'], 'L0_conv_grn_gamma': _L0_conv_in['grn_gamma'], 'L0_conv_grn_beta': _L0_conv_in['grn_beta'], 'L0_conv_w2': _L0_conv_in['w2'], 'L0_conv_b2': _L0_conv_in['b2'], 'L1_conv_weight': _L1_conv_in['weight'], 'L1_conv_bias': _L1_conv_in['bias']}

def reference(x, L0_conv_dw_w, L0_conv_dw_b, L0_conv_ln_w, L0_conv_ln_b, L0_conv_w1, L0_conv_b1, L0_conv_grn_gamma, L0_conv_grn_beta, L0_conv_w2, L0_conv_b2, L1_conv_weight, L1_conv_bias):
    import jax
    import jax.numpy as jnp

    def _L0_conv_ref(x, dw_w, dw_b, ln_w, ln_b, w1, b1, grn_gamma, grn_beta, w2, b2):
        import jax, jax.numpy as jnp
        import numpy as np
        DIM = 96
        HID = 4 * DIM
        EPS = 1e-06
        GRN_EPS = 1e-06

        def _block(x, dw_w, dw_b, ln_w, ln_b, w1, b1, grn_gamma, grn_beta, w2, b2):
            identity = x
            y = jax.lax.conv_general_dilated(x, dw_w, window_strides=(1, 1), padding=((3, 3), (3, 3)), dimension_numbers=('NCHW', 'OIHW', 'NCHW'), feature_group_count=DIM)
            y = y + dw_b[None, :, None, None]
            y = jnp.transpose(y, (0, 2, 3, 1))
            mu = jnp.mean(y, axis=-1, keepdims=True)
            var = jnp.mean(jnp.square(y - mu), axis=-1, keepdims=True)
            y = (y - mu) * jax.lax.rsqrt(var + EPS) * ln_w + ln_b
            y = jnp.einsum('bhwc,cd->bhwd', y, w1) + b1
            y = jax.nn.gelu(y, approximate=False)
            gx = jnp.sqrt(jnp.sum(jnp.square(y), axis=(1, 2), keepdims=True))
            nx = gx / (jnp.mean(gx, axis=-1, keepdims=True) + GRN_EPS)
            y = grn_gamma * (y * nx) + grn_beta + y
            y = jnp.einsum('bhwd,dc->bhwc', y, w2) + b2
            return identity + jnp.transpose(y, (0, 3, 1, 2))
        return _block(x, dw_w, dw_b, ln_w, ln_b, w1, b1, grn_gamma, grn_beta, w2, b2)

    def _L1_conv_ref(x, weight, bias):
        import jax, jax.numpy as jnp
        import numpy as np
        DIM = 96
        FRACTION = 16
        INTEGER = 16
        WEIGHT_BITS = 5
        SHIFT_MIN = -(2 ** (WEIGHT_BITS - 1) - 2)

        def _ste(x, qx):
            return x + jax.lax.stop_gradient(qx - x)

        def _clampabs(w, mn, mx):
            return jnp.sign(w) * jnp.clip(jnp.abs(w), mn, mx)

        def _round_power_of_2(w):
            shift = jnp.round(jnp.log2(jnp.maximum(jnp.abs(w), 1e-30)))
            return jnp.sign(w) * jnp.exp2(shift)

        def _round_to_fixed(x, fraction=FRACTION, integer=INTEGER):
            delta = 2.0 ** (-fraction)
            bound = 2.0 ** (integer - 1)
            return jnp.clip(jnp.floor(x / delta) * delta, -bound, bound - 1)
        w = _ste(weight, _clampabs(weight, 2.0 ** SHIFT_MIN, 1.0))
        w = _ste(w, _round_power_of_2(w))
        xq = _ste(x, _round_to_fixed(x))
        bq = _ste(bias, _round_to_fixed(bias))
        out = jax.lax.conv_general_dilated(xq, w, window_strides=(1, 1), padding=((1, 1), (1, 1)), feature_group_count=DIM, dimension_numbers=('NCHW', 'OIHW', 'NCHW'))
        return out + bq[None, :, None, None]

    def _gn(v, G=32, eps=1e-05):
        B_, C_, H_, W_ = v.shape
        g = v.reshape(B_, G, C_ // G, H_, W_)
        m = jnp.mean(g, axis=(2, 3, 4), keepdims=True)
        s = jnp.var(g, axis=(2, 3, 4), keepdims=True)
        return ((g - m) / jnp.sqrt(s + eps)).reshape(v.shape)

    def _ln_c(v, eps=1e-06):
        m = jnp.mean(v, axis=1, keepdims=True)
        s = jnp.var(v, axis=1, keepdims=True)
        return (v - m) / jnp.sqrt(s + eps)

    def _ln_t(v, eps=1e-05):
        m = jnp.mean(v, axis=-1, keepdims=True)
        s = jnp.var(v, axis=-1, keepdims=True)
        return (v - m) / jnp.sqrt(s + eps)

    def _to_tokens(v):
        B_, C_, H_, W_ = v.shape
        return v.reshape(B_, C_, H_ * W_).transpose(0, 2, 1)

    def _from_tokens(t, like):
        B_, C_, H_, W_ = like.shape
        return t.transpose(0, 2, 1).reshape(B_, C_, H_, W_)
    x = _L0_conv_ref(x, L0_conv_dw_w, L0_conv_dw_b, L0_conv_ln_w, L0_conv_ln_b, L0_conv_w1, L0_conv_b1, L0_conv_grn_gamma, L0_conv_grn_beta, L0_conv_w2, L0_conv_b2)
    x = _L1_conv_ref(x, L1_conv_weight, L1_conv_bias)
    return x

_drawn_inputs = setup_inputs


def setup_inputs(seed=0):
    import zlib

    import numpy as np

    out = dict(_drawn_inputs(seed))
    spreads = {'L0_conv_dw_b': (0.0, 0.318),
     'L0_conv_ln_w': (1.0, 0.6),
     'L0_conv_ln_b': (0.0, 0.8),
     'L0_conv_b1': (0.0, 0.329),
     'L0_conv_grn_gamma': (0.0, 0.8),
     'L0_conv_grn_beta': (0.0, 0.1),
     'L0_conv_b2': (0.0, 0.1)}
    factors = {}
    for name, (base, spread) in spreads.items():
        noise = np.random.default_rng([zlib.crc32(name.encode()), seed]).standard_normal(out[name].shape)
        drawn = base * np.exp(spread * noise) if base else spread * noise
        out[name] = jnp.asarray(drawn.astype(out[name].dtype))
    for name, factor in factors.items():
        out[name] = (out[name] * factor).astype(out[name].dtype)
    return out
```

```python
from contextlib import ExitStack

import numpy as np

import concourse.bass as bass
from concourse import mybir

ALU = mybir.AluOpType
ACT = mybir.ActivationFunctionType
AX = mybir.AxisListType
F32 = mybir.dt.float32
BF16 = mybir.dt.bfloat16
I32 = mybir.dt.int32
U32 = mybir.dt.uint32

NIMG, C, H, W = 16, 96, 56, 56
HID = 4 * C
HW = H * W
PAIR = 2 * W
NPAIR = H // 2
JP = NPAIR + 1
CB = 4
CM = CB * NPAIR
IG = 4
G = NIMG // IG
NBATCH = C // CB
NBODY = NBATCH // 2
HALO = 2
SLOTS = NPAIR + 2 * HALO
NCOL = NIMG * JP
LSTEP = 64
TW = 2 * LSTEP
LPAD = LSTEP
CH = 448
NCH = HW // CH
MT = HID // 128
FIX = 65536.0
LN_EPS = 1e-6
GRN_EPS = 1e-6
Z_USES = ((NCH + 1) // 2, NCH // 2)
LEAD = 3


def need(eng, sem, value):
    if isinstance(value, int) and value <= 0:
        return
    eng.wait_ge(sem, value)


def forwards(v, n):
    (part, (bank, _), (step, _)) = v.ap
    return bass.AP(tensor=v.tensor, offset=v.offset + LSTEP - 1,
                   ap=[part, [LSTEP, n], [bank, 2], [-1, W]])


def z_slot(p, t):
    return 2 * p + t % 2


def build(nc, x, dw_w, dw_b, ln_w, ln_b, w1, b1, grn_gamma, grn_beta, w2, b2, cw, cb, out):
    y_dram = nc.dram_tensor("y_scratch", (NIMG, C, H, W), F32)
    z_dram = nc.dram_tensor("z_scratch", (NIMG, C, H, W), F32)
    st_dram = nc.dram_tensor("stats_scratch", (6, NIMG, HW), BF16)
    lines_a = nc.dram_tensor("lines_a", (LPAD + C * TW * 4 + TW + LPAD,), F32)
    lines_c = nc.dram_tensor("lines_c", (LPAD + C * TW * 2 + TW + LPAD,), F32)

    with ExitStack() as ctx:
        def sb(name, shape, dt=F32):
            return ctx.enter_context(nc.sbuf_tensor(name, shape, dt))

        def sem(name):
            return ctx.enter_context(nc.semaphore(name))

        ident = sb("ident", [128, 128])
        ones = sb("ones", [128, 128])
        pick_m = sb("pick_m", [6, C], BF16)
        pick_r = sb("pick_r", [6, C], BF16)
        halves = sb("halves", [128, MT])
        bias_a = sb("bias_a", [TW, C])
        bias_c = sb("bias_c", [TW, C])
        rk = sb("rk", [TW, C])
        ck = sb("ck", [TW, C])
        w1s = sb("w1s", [C, HID])
        b1s = sb("b1s", [128, MT])
        b1p = sb("b1p", [128, MT])
        w2r = sb("w2r", [128, MT, C])
        w2s = sb("w2s", [128, 2, MT, C])
        gam = sb("gam", [128, MT])
        bet = sb("bet", [128, MT])
        lnw = sb("lnw", [C, 1])
        lnb = sb("lnb", [C, 1])
        b2c = sb("b2c", [C, 1])
        cvec = sb("cvec", [C, 1])
        ss = sb("ss", [128, 2, MT, NCH])
        ss3 = sb("ss3", [128, MT])
        gx = sb("gx", [128, MT])
        gsum = sb("gsum", [128, 1])
        gden = sb("gden", [128, 1])
        grec = sb("grec", [128, 1])
        gnx = sb("gnx", [128, MT])
        gsc = sb("gsc", [128, MT])

        ARENA = 43300
        arena = sb("arena", [128, ARENA])

        class Carve:
            def __init__(self):
                self.at = 0

            def __call__(self, parts, *dims):
                size = int(np.prod(dims))
                v = arena[0:parts, self.at:self.at + size]
                self.at += size
                assert self.at <= ARENA, self.at
                if len(dims) > 1:
                    names = "abcdef"[:len(dims)]
                    v = v.rearrange(f"p ({' '.join(names)}) -> p {' '.join(names)}",
                                    **{n: d for n, d in zip(names[1:], dims[1:])})
                return v

        conv = Carve()
        xin = conv(CM, 2, NIMG, PAIR)
        toep = conv(PAIR, 2, CB, 4, TW)
        xt = conv(PAIR, 2, CB, NIMG, SLOTS)
        yt = conv(TW, 2, NIMG, JP, CB)
        ost = conv(CM, 2, NIMG, PAIR)
        mean = conv(TW, NCOL)
        m2 = conv(TW, NCOL)
        dev = conv(TW, NCOL)
        dsq = conv(TW, NCOL)
        rstd = conv(TW, NCOL)
        nhalf = conv(TW, NCOL)
        mean_in = conv(TW, NIMG * NPAIR)
        rstd_in = conv(TW, NIMG * NPAIR)
        res1 = conv(IG * NPAIR, G * PAIR)
        res2 = conv(IG * NPAIR, G * PAIR)
        wa = conv(C, 49)
        wc = conv(C, 9)
        wc1 = conv(C, 9)
        wc2 = conv(C, 9)
        wc3 = conv(C, 9)
        la = conv(C, 4 * TW)
        lc = conv(C, 2 * TW)
        w1r = conv(C, HID)
        zrow = conv(1, TW + LPAD)
        bq = [conv(TW, C) for _ in range(3)]
        stb = conv(IG * NPAIR, 3 * G * PAIR).bitcast(BF16).rearrange("p (q n) -> p q n", q=6)

        mlp = Carve()
        yraw = mlp(C, 2, HW)
        yn = mlp(C, 2, HW)
        xr = mlp(C, 2, HW)
        hid = mlp(128, 2, MT, HW)
        vt = mlp(C, 2, CH)
        rt = mlp(C, 2, CH).bitcast(I32)
        dt_ = mlp(C, 2, CH)
        zt = mlp(C, 4, CH)
        sqd = mlp(128, CH // 2).bitcast(BF16)
        sqa = [mlp(128, CH // 2).bitcast(BF16) for _ in range(2)]
        rows = sb("rows", [6, 2, HW], BF16)

        BANK = 512
        psum = ctx.enter_context(nc.psum_tensor("psum", [128, 8, BANK], F32))
        bank = [psum[:, i, :] for i in range(8)]
        p_in, p_conv = bank[0:2], bank[2:4]
        p_back = [psum[:, 4:6, :], psum[:, 6:8, :]]
        p_stat = [psum[:, 0:2, :], psum[:, 2:4, :]]
        p_h, p_grn, p_mean, p_rstd, p_o = bank[0:3], bank[3], bank[4], bank[5], bank[6:8]

        small_in = sem("small_in")
        consts = sem("consts")
        prep = sem("prep")
        prep_step = sem("prep_step")
        halo = sem("halo")
        lines_made = sem("lines_made")
        lines_out = sem("lines_out")
        w1_made = sem("w1_made")
        b1_mm = sem("b1_mm")
        b1_made = sem("b1_made")
        stages = {}
        for k in "ac":
            stages[k] = {n: sem(f"{k}_{n}") for n in ("x0", "x1", "t0", "t1", "tin", "xt", "conv", "yt", "back", "out", "st0", "st1")}
        wel = sem("wel")
        var_ready = sem("var_ready")
        rstd_ready = sem("rstd_ready")
        stat_in = sem("stat_in")
        stat_t = sem("stat_t")
        stat_c = sem("stat_c")
        stat_split = sem("stat_split")
        stat_out = sem("stat_out")
        y_in = [sem("y_in0"), sem("y_in1")]
        x_in = [sem("x_in0"), sem("x_in1")]
        r_in = [sem("r_in0"), sem("r_in1")]
        bc_done = sem("bc_done")
        cen_done = sem("cen_done")
        yn_ready = sem("yn_ready")
        h_done = sem("h_done")
        gelu_done = sem("gelu_done")
        sq_act = sem("sq_act")
        sq_dve = sem("sq_dve")
        xs_ready = sem("xs_ready")
        ss_ready = sem("ss_ready")
        gx_ready = sem("gx_ready")
        gsum_done = sem("gsum_done")
        grn_step = sem("grn_step")
        w2_ready = sem("w2_ready")
        o_done = sem("o_done")
        v_ready = sem("v_ready")
        r_ready = sem("r_ready")
        clip_done = sem("clip_done")
        d_ready = sem("d_ready")
        z_ready = sem("z_ready")
        z_out = [sem(f"z_out{i}") for i in range(4)]

        def bodies(eng, body):
            body(0, True, False)
            with eng.Fori(1, NBODY - 1) as it:
                body(it, False, False)
            body(NBODY - 1, False, True)

        def steps(eng, step):
            step(0, 0)
            step(1, 1)
            step(2, 0)
            with eng.Fori(1, (NIMG - 2) // 2) as q:
                step(2 * q + 1, 1)
                step(2 * q + 2, 0)
            step(NIMG - 1, 1)
            step(NIMG, 0)

        x_v = x.rearrange("b c h w -> b c (h w)")
        y_v = y_dram.ap().rearrange("b c h w -> b c (h w)")
        z_v = z_dram.ap().rearrange("b c h w -> b c (h w)")
        out_v = out.rearrange("b c h w -> b c (h w)")
        NSMALL = 12

        block = ctx.enter_context(nc.Block())

        @block.sync
        def _(sp):
            for dst, src in ((wa, dw_w.rearrange("c o h w -> c (o h w)")),
                             (wc, cw.rearrange("c o h w -> c (o h w)")),
                             (bias_a[:, :], dw_b.rearrange("(o c) -> o c", o=1).to_broadcast([TW, C])),
                             (bq[0], cb.rearrange("(o c) -> o c", o=1).to_broadcast([TW, C])),
                             (w1r, w1),
                             (b1p[:, :], b1.rearrange("(t p) -> p t", p=128)),
                             (w2r[:, :, :], w2.rearrange("(t p) c -> p t c", p=128)),
                             (gam[:, :], grn_gamma.rearrange("(t p) -> p t", p=128)),
                             (bet[:, :], grn_beta.rearrange("(t p) -> p t", p=128)),
                             (lnw[:, :], ln_w.rearrange("(p o) -> p o", o=1)),
                             (lnb[:, :], ln_b.rearrange("(p o) -> p o", o=1)),
                             (b2c[:, :], b2.rearrange("(p o) -> p o", o=1))):
                sp.dma_start(dst, src, allow_slow_non_contiguous=True).then_inc(small_in, 16)
            sp.wait_ge(lines_made, 1)
            for n, (lines, made, kt) in enumerate(((lines_a, la, 4), (lines_c, lc, 2))):
                sp.wait_ge(lines_made, n + 1)
                end = LPAD + C * TW * kt
                sp.dma_start(lines.ap()[LPAD:end].rearrange("(c n) -> c n", c=C), made).then_inc(lines_out, 16)
                sp.dma_start(lines.ap()[0:LPAD].rearrange("(o n) -> o n", o=1), zrow[:, 0:LPAD]).then_inc(lines_out, 16)
                sp.dma_start(lines.ap()[end:end + TW + LPAD].rearrange("(o n) -> o n", o=1), zrow).then_inc(lines_out, 16)
            sp.wait_ge(lines_out, 6 * 16)

            def conv_loads(S, src, lines, kt):
                rows_of = src.rearrange("b c (m t) -> (c m) b t", t=PAIR)

                def body(it, first, last):
                    for s in range(2):
                        b = 2 * it + s
                        need(sp, S["tin"], G * (b - 1))
                        sp.dma_start(xin[:, s, :, :], rows_of[bass.ds(b * CM, CM)]).then_inc(S[f"x{s}"], 16)
                        need(sp, S["conv"], CB * (b - 1))
                        for r in range(2):
                            rows = bass.AP(tensor=lines, offset=b * (CB * kt * TW) + LPAD + r * LSTEP - (LSTEP - 1),
                                           ap=[[1, W], [TW, CB * kt], [1, TW]])
                            sp.dma_start(toep[W * r:W * r + W, s, :, 0:kt, :], rows).then_inc(S[f"t{s}"], 16)
                bodies(sp, body)

            sp.wait_ge(halo, 1)
            conv_loads(stages["a"], x_v, lines_a, 4)

            for s in range(2):
                sp.wait_ge(stages["a"][f"st{s}"], 16 * CB * NBODY)
            sp.wait_ge(stat_split, 1)
            for q in range(6):
                sp.dma_start(st_dram.ap()[q].rearrange("(g i) (m t) -> (i m) g t", i=IG, t=PAIR),
                             stb[:, q, :].rearrange("p (g t) -> p g t", g=G)).then_inc(stat_out, 16)
            sp.wait_ge(stat_out, 6 * 16)

            def load_y(i, p):
                need(sp, yn_ready, NCH * (i - 1))
                sp.dma_start(yraw[:, p, :], y_v[i]).then_inc(y_in[p], 16)
                sp.dma_start(rows[:, p, :], st_dram.ap().rearrange("q i t -> i q t")[i]).then_inc(r_in[p], 16)

            def load_x(i, p):
                need(sp, v_ready, NCH * (i - 1))
                sp.dma_start(xr[:, p, :], x_v[i]).then_inc(x_in[p], 16)

            def stores(i, p):
                for t in range(NCH):
                    sp.wait_ge(z_ready, NCH * i + t + 1)
                    sp.dma_start(z_v[i][:, CH * t:CH * t + CH], zt[:, z_slot(p, t), :]).then_inc(z_out[z_slot(p, t)], 16)

            def step(i, p, more_y=True, more_x=True):
                if more_y:
                    load_y(i + 2, p)
                stores(i - 1, 1 - p)
                if more_x:
                    load_x(i + 1, 1 - p)

            load_y(0, 0)
            load_y(1, 1)
            load_x(0, 0)
            load_x(1, 1)
            load_y(2, 0)
            with sp.Fori(0, (NIMG - 4) // 2) as q:
                step(2 * q + 1, 1)
                step(2 * q + 2, 0)
            step(NIMG - 3, 1)
            step(NIMG - 2, 0, more_y=False)
            step(NIMG - 1, 1, more_y=False, more_x=False)
            step(NIMG, 0, more_y=False, more_x=False)
            for k in range(4):
                sp.wait_ge(z_out[k], 16 * Z_USES[k % 2] * NIMG // 2)
            sp.wait_ge(halo, 2)
            conv_loads(stages["c"], z_v, lines_c, 2)
            for s in range(2):
                sp.wait_ge(stages["c"][f"st{s}"], 16 * CB * NBODY)

        @block.gpsimd
        def _(pool):
            pool.memset(ident[:, :], 0.0).then_inc(prep, 1)
            pool.iota(rk[:, :].bitcast(I32), pattern=[[1, C]], base=1, channel_multiplier=0).then_inc(prep, 1)
            pool.memset(ones[:, :], 1.0).then_inc(consts, 1)
            pool.memset(pick_m[:, :], 0.0).then_inc(prep, 1)
            pool.memset(pick_r[:, :], 1.0).then_inc(prep, 1)
            pool.memset(halves[:, :], 0.5).then_inc(consts, 1)
            pool.memset(nhalf, -0.5).then_inc(consts, 1)
            pool.wait_ge(prep, 4)
            pool.memset(pick_m[0:3, :], 1.0).then_inc(consts, 1)
            pool.memset(pick_r[0:3, :], 0.0).then_inc(consts, 1)
            pool.affine_select(out=ident[:, :], in_=ident[:, :], compare_op=ALU.not_equal, fill=1.0,
                               base=0, pattern=[[-1, 128]], channel_multiplier=1).then_inc(consts, 1)
            pool.wait_ge(var_ready, 1)
            pool.tensor_tensor(rstd, dsq, nhalf, ALU.pow).then_inc(rstd_ready, 1)

            def step(i, p):
                if not (isinstance(i, int) and i == 0):
                    pool.wait_ge(ss_ready, i)
                    pool.tensor_tensor(gx[:, :], ss3[:, :], halves[:, :], ALU.pow).then_inc(gx_ready, 1)
            steps(pool, step)

        @block.tensor
        def _(pe):
            pe.wait_ge(consts, 6)
            pe.wait_ge(small_in, 16 * NSMALL)
            for t in range(MT):
                nc.tensor.matmul(bank[6][:, t:t + 1], w1r[:, 128 * t:128 * t + 128], lnb[:, :], start=(t == 0), stop=(t == MT - 1), skip_group_check=True)
            for t in range(MT):
                mm = nc.tensor.matmul(bank[7][0:C, 0:1], w2r[:, t, :], bet[:, t:t + 1], start=(t == 0), stop=(t == MT - 1))
            mm.then_inc(b1_mm, 1)

            def conv_stage(S, kt, slot0):
                def tin(b, s, p):
                    n = G * b + s
                    if s == 0:
                        pe.wait_ge(S[f"x{p}"], 8 * (b - p) + 16)
                    need(pe, S["xt"], n - 1)
                    for i in range(IG):
                        mm = nc.tensor.transpose(p_in[s % 2][0:PAIR, CM * i:CM * i + CM], xin[:, p, IG * s + i, :], ident[0:CM, 0:CM])
                    mm.then_inc(S["tin"], 1)

                def convolve(b, s, p, then_back):
                    n = CB * b + s
                    if s == 0:
                        pe.wait_ge(S[f"t{p}"], 16 * (b - p) + 32)
                        pe.wait_ge(S["xt"], G * b + G)
                    need(pe, S["yt"], n - 1)
                    for k in range(kt):
                        if then_back and k == kt - 1:
                            back_waits(b - 1, s)
                        mm = nc.tensor.matmul(p_conv[s % 2][:, 0:NCOL], toep[:, p, s, k, :],
                                              xt[:, p, s, :, slot0 + k:slot0 + k + JP], start=(k == 0), stop=(k == kt - 1))
                    mm.then_inc(S["conv"], 1)

                def back_waits(b, s):
                    if s == 0:
                        pe.wait_ge(S["yt"], CB * b + CB)
                    need(pe, S["out"], G * b + s - 1)

                def back(b, s, p):
                    for i in range(IG):
                        cols = yt[:, p, IG * s + i, :, :]
                        for r in range(2):
                            q = LSTEP * (1 - r)
                            mm = nc.tensor.transpose(p_back[s % 2][0:CM, 1 - r, LSTEP * i:LSTEP * i + LSTEP],
                                                     cols[q:q + LSTEP, 1 - r:1 - r + NPAIR, :].rearrange("p m c -> p (m c)"),
                                                     ident[q:q + LSTEP, q:q + LSTEP])
                    mm.then_inc(S["back"], 1)

                for s in range(G):
                    tin(0, s, 0)

                def body(it, first, last):
                    for p in range(2):
                        b = 2 * it + p
                        for s in range(G):
                            if not (last and p == 1):
                                tin(b + 1, s, 1 - p)
                            convolve(b, s, p, not (first and p == 0))
                            if not (first and p == 0):
                                back(b - 1, s, 1 - p)
                bodies(pe, body)
                for s in range(G):
                    back_waits(NBATCH - 1, s)
                    back(NBATCH - 1, s, 1)

            pe.wait_ge(b1_made, 2)
            conv_stage(stages["a"], 4, 0)

            pe.wait_ge(stages["a"]["out"], C)
            pe.wait_ge(stat_in, 1)
            for q, v in enumerate((mean_in, rstd_in)):
                for g in range(G):
                    for r in range(2):
                        a = LSTEP * (1 - r)
                        mm = nc.tensor.transpose(p_stat[q][0:IG * NPAIR, 1 - r, LSTEP * g:LSTEP * g + LSTEP],
                                                 v[a:a + LSTEP, IG * NPAIR * g:IG * NPAIR * (g + 1)], ident[a:a + LSTEP, a:a + LSTEP])
            mm.then_inc(stat_t, 1)
            pe.wait_ge(stat_split, 1)

            def bcast(i, p, t):
                if t == 0:
                    pe.wait_ge(r_in[p], 8 * (i - p) + 16)
                need(pe, yn_ready, NCH * i + t)
                nc.tensor.matmul(p_mean[0:C, 0:CH], pick_m[:, :], rows[:, p, CH * t:CH * t + CH], start=True, stop=True)
                nc.tensor.matmul(p_rstd[0:C, 0:CH], pick_r[:, :], rows[:, p, CH * t:CH * t + CH], start=True, stop=True).then_inc(bc_done, 1)

            def up(i, p, t):
                pe.wait_ge(yn_ready, NCH * i + t + 1)
                for m in range(MT):
                    need(pe, gelu_done, MT * (NCH * i + t) + m + 1 - MT)
                    nc.tensor.matmul(p_h[m][:, 0:CH], w1s[:, 128 * m:128 * m + 128], yn[:, p, CH * t:CH * t + CH],
                                     start=True, stop=True).then_inc(h_done, 1)

            def down(i, p, t):
                if t == 0:
                    pe.wait_ge(w2_ready, i + 1)
                need(pe, v_ready, NCH * i + t - 1)
                k = (t + p) % 2
                for m in range(MT):
                    mm = nc.tensor.matmul(p_o[k][0:C, 0:CH], w2s[:, p, m, :], hid[:, p, m, CH * t:CH * t + CH],
                                          start=(m == 0), stop=(m == MT - 1))
                mm.then_inc(o_done, 1)

            def step(i, p):
                fixed = isinstance(i, int)
                head, tail = fixed and i == 0, fixed and i == NIMG
                ahead = not (fixed and i >= NIMG - 1)
                for t in range(NCH + LEAD):
                    if t < NCH and ahead:
                        bcast(i + 1, 1 - p, t)
                    if t < NCH and not tail:
                        up(i, p, t)
                    if t == 1 and not head:
                        pe.wait_ge(gx_ready, i)
                        nc.tensor.matmul(p_grn[:, 0:MT], ones[:, :], gx[:, :], start=True, stop=True).then_inc(gsum_done, 1)
                    if t >= LEAD and not head:
                        down(i - 1, 1 - p, t - LEAD)

            for t in range(NCH):
                bcast(0, 0, t)
            steps(pe, step)
            pe.wait_ge(v_ready, NCH * NIMG)
            conv_stage(stages["c"], 2, 1)

        @block.scalar
        def _(act):
            act.wait_ge(small_in, 16 * NSMALL)
            act.wait_ge(halo, 1)

            def conv_stage(S, dst, bias, scale):
                rows_of = dst.rearrange("b c (m t) -> (c m) b t", t=PAIR)

                def xt_copy(b, s, p):
                    act.wait_ge(S["tin"], G * b + s + 1)
                    if s == 0:
                        need(act, S["conv"], CB * (b - 1))
                    nc.scalar.activation(xt[:, p, :, IG * s:IG * s + IG, HALO:HALO + NPAIR].rearrange("p c i m -> p i c m"),
                                         p_in[s % 2][0:PAIR, 0:IG * CM].rearrange("p (i c m) -> p i c m", i=IG, c=CB),
                                         ACT.Identity).then_inc(S["xt"], 1)

                def yt_copy(b, s, p):
                    n = CB * b + s
                    act.wait_ge(S["conv"], n + 1)
                    if s == 0:
                        need(act, S["back"], G * (b - 1))
                    if S is stages["a"]:
                        need(act, wel, 4 * (n - 2 * CB) + 4)
                    nc.scalar.activation(yt[:, p, :, :, s], p_conv[s % 2][:, 0:NCOL].rearrange("p (i j) -> p i j", i=NIMG), ACT.Identity,
                                         bias=bias[:, bass.ds(n, 1)], scale=scale).then_inc(S["yt"], 1)

                def out_copy(b, s, p):
                    n = G * b + s
                    act.wait_ge(S["back"], n + 1)
                    if s == 0:
                        need(act, S[f"st{p}"], 8 * CB * (b - p))
                    nc.scalar.activation(ost[:, p, IG * s:IG * s + IG, :].rearrange("p i (h w) -> p i h w", h=2),
                                         forwards(p_back[s % 2][0:CM], IG),
                                         ACT.Identity).then_inc(S["out"], 1)
                    if s == G - 1:
                        act.wait_ge(S["out"], n + 1)
                        for c in range(CB):
                            act.dma_start(rows_of[bass.ds(b * CM + NPAIR * c, NPAIR)],
                                          ost[c:CM:CB, p, :, :]).then_inc(S[f"st{p}"], 16)

                for s in range(G):
                    xt_copy(0, s, 0)

                def body(it, first, last):
                    for p in range(2):
                        b = 2 * it + p
                        for s in range(G):
                            if not (last and p == 1):
                                xt_copy(b + 1, s, 1 - p)
                            yt_copy(b, s, p)
                            if not (first and p == 0):
                                out_copy(b - 1, s, 1 - p)
                bodies(act, body)
                for s in range(G):
                    out_copy(NBATCH - 1, s, 1)

            conv_stage(stages["a"], y_v, bias_a, 1.0)

            act.wait_ge(b1_made, 2)

            def step(i, p):
                fixed = isinstance(i, int)
                head, tail = fixed and i == 0, fixed and i == NIMG
                for t in range(NCH + LEAD):
                    if t < NCH and not tail:
                        if t == 0:
                            need(act, o_done, NCH * (i - 1))
                        for m in range(MT):
                            n = MT * (NCH * i + t) + m
                            act.wait_ge(h_done, n + 1)
                            nc.scalar.activation(hid[:, p, m, CH * t:CH * t + CH], p_h[m][:, 0:CH], ACT.Gelu,
                                                 bias=b1s[:, m:m + 1]).then_inc(gelu_done, 1)
                        for m in range(2):
                            n = MT * (NCH * i + t) + m
                            act.wait_ge(gelu_done, n + 1)
                            need(act, sq_act, 2 * (NCH * i + t) + m - 1)
                            nc.scalar.activation(sqa[m], hid[:, p, m, CH * t:CH * t + CH], ACT.Square,
                                                 accum_out=ss[:, p, m, t:t + 1]).then_inc(sq_act, 1)
                    if t >= LEAD - 1 and t < NCH + LEAD - 1 and not head:
                        k = t - LEAD + 1
                        if k == 0:
                            act.wait_ge(x_in[1 - p], 8 * (i - 2 + p) + 16)
                        xc = xr[:, 1 - p, CH * k:CH * k + CH]
                        nc.scalar.activation(xc, xc, ACT.Identity, bias=cvec[:, :], scale=FIX).then_inc(xs_ready, 1)
            steps(act, step)
            act.wait_ge(halo, 2)
            conv_stage(stages["c"], out_v, bias_c, -1.0 / FIX)

        @block.vector
        def _(dve):
            chain_sem = prep_step
            chain = [0]

            def link(ins):
                chain[0] += 1
                ins.then_inc(chain_sem, 1)
                dve.wait_ge(chain_sem, chain[0])

            def clear_halos():
                return dve.memset(xt.rearrange("p a b c d -> p (a b c d)"), 0.0)

            link(clear_halos())
            dve.memset(mean, 0.0)
            dve.memset(m2, 0.0)
            dve.memset(la, 0.0)
            dve.memset(zrow, 0.0)
            link(dve.memset(lc, 0.0))
            dve.sem_inc(halo, 1)
            dve.wait_ge(prep, 2)
            link(dve.tensor_copy(ck[:, :], rk[:, :].bitcast(I32)))
            link(dve.reciprocal(rk[:, :], ck[:, :]))
            link(dve.tensor_scalar(ck[:, :], rk[:, :], -1.0, 1.0, ALU.mult, ALU.add))
            dve.wait_ge(small_in, 16 * NSMALL)
            for dy in range(7):
                for dx in range(7):
                    at = (dy + 1) * LSTEP + dx - 3
                    ins = dve.tensor_copy(la[:, at:at + 1], wa[:, 7 * dy + dx:7 * dy + dx + 1])
            link(ins)
            dve.sem_inc(lines_made, 1)
            link(dve.tensor_scalar(wc1.bitcast(U32), wc.bitcast(U32), 0x7FFFFFFF, None, ALU.bitwise_and))
            link(dve.tensor_scalar(wc1, wc1, 2.0 ** -14, 1.0, ALU.max, ALU.min))
            link(dve.tensor_scalar(wc2.bitcast(U32), wc.bitcast(U32), 0x80000000, None, ALU.bitwise_and))
            link(dve.tensor_tensor(wc1.bitcast(U32), wc1.bitcast(U32), wc2.bitcast(U32), ALU.bitwise_or))
            link(dve.tensor_scalar(wc2, wc, 0.0, None, ALU.not_equal))
            link(dve.tensor_tensor(wc1, wc1, wc2, ALU.mult))
            link(dve.tensor_tensor(wc1, wc1, wc, ALU.subtract))
            link(dve.tensor_tensor(wc1, wc1, wc, ALU.add))
            link(dve.tensor_scalar(wc2, wc1, float(np.sqrt(2.0)), None, ALU.mult))
            link(dve.tensor_scalar(wc3.bitcast(U32), wc2.bitcast(U32), 0xFF800000, None, ALU.bitwise_and))
            link(dve.tensor_tensor(wc3, wc3, wc1, ALU.subtract))
            link(dve.tensor_tensor(wc3, wc3, wc1, ALU.add))
            for dy in range(3):
                for dx in range(3):
                    at = (dy + 1) * LSTEP + dx - 1
                    ins = dve.tensor_copy(lc[:, at:at + 1], wc3[:, 3 * dy + dx:3 * dy + dx + 1])
            link(ins)
            dve.sem_inc(lines_made, 1)
            link(dve.tensor_scalar(bq[1], bq[0], FIX, FIX * 32767.0, ALU.mult, ALU.min))
            link(dve.tensor_scalar(bq[1], bq[1], -FIX * 32768.0, None, ALU.max))
            link(dve.tensor_copy(bq[2].bitcast(I32), bq[1]))
            link(dve.tensor_tensor(bq[1], bq[1], bq[2].bitcast(I32), ALU.subtract))
            link(dve.scalar_tensor_tensor(out=bq[1], in0=bq[1], scalar=0.0, in1=bq[2].bitcast(I32), op0=ALU.is_lt, op1=ALU.subtract))
            link(dve.scalar_tensor_tensor(out=bq[1], in0=bq[1], scalar=-1.0 / FIX, in1=bq[0], op0=ALU.mult, op1=ALU.subtract))
            link(dve.tensor_tensor(bias_c[:, :], bq[1], bq[0], ALU.add))
            link(dve.tensor_scalar(w1s[:, :], w1r, lnw[:, 0:1], None, ALU.mult))
            dve.wait_ge(b1_mm, 1)
            dve.tensor_tensor(b1s[:, :], bank[6][:, 0:MT], b1p[:, :], ALU.add).then_inc(b1_made, 1)
            link(dve.tensor_tensor(cvec[:, :], bank[7][0:C, 0:1], b2c[:, :], ALU.add))
            dve.tensor_scalar(cvec[:, :], cvec[:, :], FIX, None, ALU.mult).then_inc(b1_made, 1)

            A = stages["a"]

            def grid(v):
                return v.rearrange("p (i j) -> p i j", i=NIMG)

            def update(n, p, s):
                dve.wait_ge(A["yt"], n + 1)
                need(dve, wel, 4 * n)
                dve.tensor_tensor(grid(dev), yt[:, p, :, :, s], grid(mean), ALU.subtract).then_inc(wel, 1)
                dve.wait_ge(wel, 4 * n + 1)
                dve.scalar_tensor_tensor(out=mean, in0=dev, scalar=rk[:, bass.ds(n, 1)], in1=mean, op0=ALU.mult, op1=ALU.add).then_inc(wel, 1)
                dve.scalar_tensor_tensor(out=dsq, in0=dev, scalar=ck[:, bass.ds(n, 1)], in1=dev, op0=ALU.mult, op1=ALU.mult).then_inc(wel, 1)
                dve.wait_ge(wel, 4 * n + 3)
                dve.tensor_tensor(m2, m2, dsq, ALU.add).then_inc(wel, 1)

            def body(it, first, last):
                for p in range(2):
                    for s in range(CB):
                        update(CB * (2 * it + p) + s, p, s)
            bodies(dve, body)

            dve.wait_ge(wel, 4 * C)
            dve.tensor_scalar(dsq, m2, 1.0 / C, LN_EPS, ALU.mult, ALU.add).then_inc(var_ready, 1)
            def inside(to, v):
                to = to.rearrange("p (i m) -> p i m", i=NIMG)
                dve.tensor_copy(to[0:LSTEP], grid(v)[0:LSTEP, :, 0:NPAIR])
                return dve.tensor_copy(to[LSTEP:TW], grid(v)[LSTEP:TW, :, 1:JP])
            inside(mean_in, mean)
            dve.wait_ge(rstd_ready, 1)
            inside(rstd_in, rstd).then_inc(stat_in, 1)
            dve.wait_ge(stat_t, 1)
            for q in range(2):
                v = forwards(p_stat[q][0:IG * NPAIR], G)
                link(dve.tensor_copy(res1.rearrange("p (g h w) -> p g h w", g=G, h=2), v))
                link(dve.tensor_copy(stb[:, 3 * q, :], res1))
                link(dve.tensor_tensor(res2, res1, stb[:, 3 * q, :], ALU.subtract))
                link(dve.tensor_copy(stb[:, 3 * q + 1, :], res2))
                link(dve.tensor_tensor(res1, res2, stb[:, 3 * q + 1, :], ALU.subtract))
                link(dve.tensor_copy(stb[:, 3 * q + 2, :], res1))
            dve.sem_inc(stat_split, 1)

            def normalise(i, p, t):
                dve.wait_ge(bc_done, NCH * i + t + 1)
                if t == 0:
                    dve.wait_ge(y_in[p], 8 * (i - p) + 16)
                    need(dve, h_done, MT * NCH * (i - 1))
                yc = yraw[:, p, CH * t:CH * t + CH]
                dve.tensor_tensor(yc, yc, p_mean[0:C, 0:CH], ALU.subtract).then_inc(cen_done, 1)
                dve.wait_ge(cen_done, NCH * i + t + 1)
                dve.tensor_tensor(yn[:, p, CH * t:CH * t + CH], yc, p_rstd[0:C, 0:CH], ALU.mult).then_inc(yn_ready, 1)

            def squares(i, p, t):
                dve.wait_ge(gelu_done, MT * (NCH * i + t) + MT)
                need(dve, sq_dve, NCH * i + t)
                hc = hid[:, p, 2, CH * t:CH * t + CH]
                dve.tensor_tensor_reduce(out=sqd, in0=hc, in1=hc, scale=1.0, scalar=0.0, op0=ALU.mult, op1=ALU.add,
                                         accum_out=ss[:, p, 2, t:t + 1]).then_inc(sq_dve, 1)

            def grn_sums(i, p):
                dve.wait_ge(sq_act, 2 * NCH * (i + 1))
                dve.wait_ge(sq_dve, NCH * (i + 1))
                dve.tensor_reduce(ss3[:, :], ss[:, p, :, :], AX.X, ALU.add).then_inc(ss_ready, 1)

            def grn_scale(i, p):
                n = 5 * i
                dve.wait_ge(gsum_done, i + 1)
                dve.tensor_reduce(gsum[:, :], p_grn[:, 0:MT], AX.X, ALU.add).then_inc(grn_step, 1)
                dve.wait_ge(grn_step, n + 1)
                dve.tensor_scalar(gden[:, :], gsum[:, :], 1.0 / HID, GRN_EPS, ALU.mult, ALU.add).then_inc(grn_step, 1)
                dve.wait_ge(grn_step, n + 2)
                dve.reciprocal(grec[:, :], gden[:, :]).then_inc(grn_step, 1)
                dve.wait_ge(grn_step, n + 3)
                dve.scalar_tensor_tensor(out=gnx[:, :], in0=gx[:, :], scalar=grec[:, 0:1], in1=gam[:, :], op0=ALU.mult, op1=ALU.mult).then_inc(grn_step, 1)
                dve.wait_ge(grn_step, n + 4)
                dve.tensor_scalar(gsc[:, :], gnx[:, :], FIX, FIX, ALU.mult, ALU.add).then_inc(grn_step, 1)
                dve.wait_ge(grn_step, n + 5)
                for m in range(MT):
                    ins = dve.tensor_scalar(w2s[:, p, m, :], w2r[:, m, :], gsc[:, m:m + 1], None, ALU.mult)
                ins.then_inc(w2_ready, 1)

            def quantise(i, p, t):
                n = NCH * i + t
                k = (t + p) % 2
                dve.wait_ge(o_done, n + 1)
                dve.wait_ge(xs_ready, n + 1)
                dve.tensor_tensor(vt[:, k, :], p_o[k][0:C, 0:CH], xr[:, p, CH * t:CH * t + CH], ALU.add).then_inc(v_ready, 1)
                dve.wait_ge(v_ready, n + 1)
                dve.tensor_scalar(vt[:, k, :], vt[:, k, :], FIX * 32767.0, -FIX * 32768.0, ALU.min, ALU.max).then_inc(clip_done, 1)
                dve.wait_ge(clip_done, n + 1)
                dve.tensor_copy(rt[:, k, :], vt[:, k, :]).then_inc(r_ready, 1)

            def floor_of(i, p, t):
                n = NCH * i + t
                k = (t + p) % 2
                j = z_slot(p, t)
                dve.wait_ge(r_ready, n + 1)
                dve.tensor_tensor(dt_[:, k, :], vt[:, k, :], rt[:, k, :], ALU.subtract).then_inc(d_ready, 1)
                dve.wait_ge(d_ready, n + 1)
                need(dve, z_out[j], 8 * Z_USES[t % 2] * (i - p) + 16 * (t // 2))
                dve.scalar_tensor_tensor(out=zt[:, j, :], in0=dt_[:, k, :], scalar=0.0, in1=rt[:, k, :],
                                         op0=ALU.is_lt, op1=ALU.subtract).then_inc(z_ready, 1)

            def step(i, p):
                fixed = isinstance(i, int)
                head, tail = fixed and i == 0, fixed and i == NIMG
                ahead = not (fixed and i >= NIMG - 1)
                for t in range(NCH + LEAD):
                    if t == 0 and not head:
                        grn_sums(i - 1, 1 - p)
                    if t < NCH and ahead:
                        normalise(i + 1, 1 - p, t)
                    if t == 1 and not head:
                        grn_scale(i - 1, 1 - p)
                    if t < NCH and not tail:
                        squares(i, p, t)
                    if t >= LEAD and not head:
                        quantise(i - 1, 1 - p, t - LEAD)
                        if t > LEAD:
                            floor_of(i - 1, 1 - p, t - LEAD - 1)
                if not head:
                    floor_of(i - 1, 1 - p, NCH - 1)

            for t in range(NCH):
                normalise(0, 0, t)
            steps(dve, step)
            dve.wait_ge(z_ready, NCH * NIMG)
            for k in range(4):
                dve.wait_ge(z_out[k], 16 * Z_USES[k % 2] * NIMG // 2)
            dve.wait_ge(sq_act, 2 * NCH * NIMG)
            link(clear_halos())
            dve.sem_inc(halo, 1)


_INS = ["x", "L0_conv_dw_w", "L0_conv_dw_b", "L0_conv_ln_w", "L0_conv_ln_b", "L0_conv_w1", "L0_conv_b1",
        "L0_conv_grn_gamma", "L0_conv_grn_beta", "L0_conv_w2", "L0_conv_b2", "L1_conv_weight", "L1_conv_bias"]


def kernel(**inputs):
    import numpy as _np
    import concourse.bacc as _bacc
    from concourse import mybir as _mybir
    from concourse.bass_utils import run_bass_kernel_spmd as _run

    nc = _bacc.Bacc("TRN2", target_bir_lowering=False, num_devices=1)
    arrays, args = {}, []
    for name in _INS:
        a = _np.ascontiguousarray(inputs[name])
        arrays[f"in_{name}_dram"] = a
        args.append(nc.dram_tensor(f"in_{name}_dram", a.shape, _mybir.dt.from_np(a.dtype), kind="ExternalInput").ap())
    args.append(nc.dram_tensor("out_0_dram", (NIMG, C, H, W), F32, kind="ExternalOutput").ap())
    build(nc, *args)
    r = _run(nc, [arrays], core_ids=[0])
    return r.results[0]["out_0_dram"]
```

```python
from contextlib import ExitStack

import numpy as np

import concourse.bass as bass
from concourse import mybir

ALU = mybir.AluOpType
ACT = mybir.ActivationFunctionType
AX = mybir.AxisListType
F32 = mybir.dt.float32
F32R = mybir.dt.float32r
BF16 = mybir.dt.bfloat16
I32 = mybir.dt.int32
U32 = mybir.dt.uint32

NIMG, C, H, W = 16, 96, 56, 56
HID = 4 * C
HW = H * W
PAIR = 2 * W
NPAIR = H // 2
JP = NPAIR + 1
CB = 4
RUN = 4 * W
NRUN = H // 4
CR = CB * NRUN
CM = 2 * CR
NI2 = NIMG // 2
IG = 4
G = NIMG // IG
NBATCH = C // CB
NBODY = NBATCH // 2
HALO = 2
SLOTS = NPAIR + 2 * HALO
NPIX = NIMG * NPAIR
NCOL = NIMG * JP
LSTEP = 64
TW = 2 * LSTEP
LPAD = LSTEP
CH = 448
NCH = HW // CH
MT = HID // 128
FIX = 65536.0
LN_EPS = 1e-6
GRN_EPS = 1e-6
Z_USES = ((NCH + 1) // 2, NCH // 2)
LEAD = 2
BLEAD = 1


SQ_SPLIT = 4
SQ_WIDE = SQ_SPLIT * CH


def need(eng, sem, value):
    if isinstance(value, int) and value <= 0:
        return
    eng.wait_ge(sem, value)


def forwards(v, n):
    (part, (bank, _), (step, _)) = v.ap
    return bass.AP(tensor=v.tensor, offset=v.offset + LSTEP - 1,
                   ap=[part, [LSTEP, n], [bank, 2], [-1, W]])


def z_slot(p, t):
    return 2 * p + t % 2


def build(nc, x, dw_w, dw_b, ln_w, ln_b, w1, b1, grn_gamma, grn_beta, w2, b2, cw, cb, out):
    y_dram = nc.dram_tensor("y_scratch", (NIMG, C, H, W), F32)
    z_dram = nc.dram_tensor("z_scratch", (NIMG, C, H, W), F32)
    st_dram = nc.dram_tensor("stats_scratch", (6, NIMG, HW), BF16)
    lines_a = [nc.dram_tensor(f"lines_a{n}", (LPAD + C * TW * 4 + TW + LPAD,), F32) for n in range(2)]
    lines_c = [nc.dram_tensor("lines_c", (LPAD + C * TW * 2 + TW + LPAD,), F32)]

    with ExitStack() as ctx:
        def sb(name, shape, dt=F32):
            return ctx.enter_context(nc.sbuf_tensor(name, shape, dt))

        def sem(name):
            return ctx.enter_context(nc.semaphore(name))

        ident = sb("ident", [128, 128])
        ones = sb("ones", [128, 128])
        pick_m = sb("pick_m", [6, C], BF16)
        pick_r = sb("pick_r", [6, C], BF16)
        halves = sb("halves", [128, MT])
        bias_a = sb("bias_a", [TW, C])
        bias_c = sb("bias_c", [TW, C])
        rk = sb("rk", [TW, C])
        ck = sb("ck", [TW, C])
        w1h = sb("w1h", [C + 1, HID], F32R)
        w1l = sb("w1l", [C + 1, HID], F32R)
        w2r = sb("w2r", [128, MT, C])
        w2s = sb("w2s", [128, 2, MT, C])
        gam = sb("gam", [128, MT])
        bet = sb("bet", [128, MT])
        lnw = sb("lnw", [C, 1])
        lnb = sb("lnb", [C, 1])
        b2c = sb("b2c", [C, 1])
        cvec = sb("cvec", [C, 1])
        ss = sb("ss", [128, 2, MT, 2])
        ss3 = sb("ss3", [128, MT])
        gx = sb("gx", [128, MT])
        gsum = sb("gsum", [128, 1])
        gden = sb("gden", [128, 1])
        grec = sb("grec", [128, 1])
        gnx = sb("gnx", [128, MT])
        gsc = sb("gsc", [128, MT])

        ARENA, ARENA_R = 28672, 16384
        arena = sb("arena", [128, ARENA])
        arena_r = sb("arena_r", [128, ARENA_R], F32R)

        class Carve:
            def __init__(self, region, limit):
                self.region, self.limit, self.at = region, limit, 0

            def __call__(self, parts, *dims):
                size = int(np.prod(dims))
                v = self.region[0:parts, self.at:self.at + size]
                self.at += size
                assert self.at <= self.limit, self.at
                if len(dims) > 1:
                    names = "abcdef"[:len(dims)]
                    v = v.rearrange(f"p ({' '.join(names)}) -> p {' '.join(names)}",
                                    **{n: d for n, d in zip(names[1:], dims[1:])})
                return v

        conv, conv_r = Carve(arena, ARENA), Carve(arena_r, ARENA_R)
        xin = conv(CM, 2, NI2, RUN)
        toep_h = conv_r(PAIR, 2, CB, 4, TW)
        toep_l = conv_r(PAIR, 2, CB, 4, TW)
        xt_h = conv_r(PAIR, 2, CB, SLOTS, NIMG)
        xt_l = conv_r(PAIR, 2, CB, SLOTS, NIMG)
        yt = conv(TW, 2, NI2, 2, 2, CB * NRUN)
        ost = conv(CM, 2, NI2, RUN)
        mean = conv(TW, NPIX)
        m2 = conv(TW, NPIX)
        dev = conv(TW, NPIX)
        dsq = conv(TW, 2, NPIX)
        rstd = conv(TW, NPIX)
        var = conv(TW, NPIX)
        root = conv(TW, NPIX)
        mean_in = conv(TW, NPIX)
        rstd_in = conv(TW, NPIX)
        res1 = conv(IG * NPAIR, G * PAIR)
        res2 = conv(IG * NPAIR, G * PAIR)
        wa = conv(C, 49)
        wc = conv(C, 9)
        wc1 = conv(C, 9)
        wc2 = conv(C, 9)
        wc3 = conv(C, 9)
        la = conv(C, 4 * TW)
        la_h = conv(C, 4 * TW)
        la_l = conv(C, 4 * TW)
        lc = conv(C, 2 * TW)
        w1r = conv(C + 1, HID)
        w1g = conv(C + 1, HID)
        lnb_last = conv(C, C + 1)
        zrow = conv(1, TW + LPAD)
        bq = [conv(TW, C) for _ in range(3)]
        stb = conv(IG * NPAIR, 3 * G * PAIR).bitcast(BF16).rearrange("p (q n) -> p q n", q=6)

        mlp, mlp_r = Carve(arena, ARENA), Carve(arena_r, ARENA_R)
        yraw = mlp_r(C, 2, HW).bitcast(F32)
        rows = mlp_r(6, HW).bitcast(BF16).rearrange("q (s n) -> q s n", s=2)
        yh = mlp_r(C + 1, HW)
        yl = mlp_r(C + 1, HW)
        ct = mlp(C, 3, CH)
        xr = mlp(C, HW)
        hid = mlp(128, 2, MT, HW)
        vt = mlp(C, 2, CH)
        rt = mlp(C, 2, CH).bitcast(I32)
        dt_ = mlp(C, 2, CH)
        zt = mlp(C, 4, CH)
        sqd = mlp(128, SQ_WIDE // 2).bitcast(BF16)

        BANK = 512
        psum = ctx.enter_context(nc.psum_tensor("psum", [128, 8, BANK], F32))
        bank = [psum[:, i, :] for i in range(8)]
        p_in, p_conv = bank[0:2], bank[2:4]
        p_back = [psum[:, 4:6, :], psum[:, 6:8, :]]
        p_stat = [psum[:, 0:2, :], psum[:, 2:4, :]]
        p_h, p_mean, p_rstd, p_o = bank[0:3], bank[3:5], bank[5], bank[6:8]
        p_grn = [b[:, CH:CH + MT] for b in p_o]

        small_in = sem("small_in")
        consts = sem("consts")
        prep = sem("prep")
        prep_step = sem("prep_step")
        halo = sem("halo")
        lines_made = sem("lines_made")
        lines_out = sem("lines_out")
        w1_made = sem("w1_made")
        b1_mm = sem("b1_mm")
        b1_made = sem("b1_made")
        stages = {}
        for k in "ac":
            stages[k] = {n: sem(f"{k}_{n}") for n in ("x0", "x1", "t0", "t1", "tin", "xh", "xt", "conv", "yt", "back", "out", "st0", "st1")}
        wel = sem("wel")
        m2_done = sem("m2_done")
        var_ready = sem("var_ready")
        root_ready = sem("root_ready")
        ones_row = sem("ones_row")
        stat_in = sem("stat_in")
        stat_t = sem("stat_t")
        stat_c = sem("stat_c")
        stat_split = sem("stat_split")
        stat_out = sem("stat_out")
        y_in = [sem("y_in0"), sem("y_in1")]
        x_in = [sem(f"x_in{t}") for t in range(NCH)]
        r_in = [sem("r_in0"), sem("r_in1")]
        bc_done = sem("bc_done")
        cen_done = sem("cen_done")
        scale_done = sem("scale_done")
        yh_ready = sem("yh_ready")
        yn_ready = sem("yn_ready")
        h_done = sem("h_done")
        gelu_done = sem("gelu_done")
        sq_act = sem("sq_act")
        ss_ready = sem("ss_ready")
        gx_ready = sem("gx_ready")
        gsum_done = sem("gsum_done")
        grn_step = sem("grn_step")
        w2_ready = sem("w2_ready")
        o_done = sem("o_done")
        v_ready = sem("v_ready")
        r_ready = sem("r_ready")
        d_ready = sem("d_ready")
        z_ready = sem("z_ready")
        z_out = [sem(f"z_out{i}") for i in range(4)]

        def tile_group(v, p, s, h):
            return v[:, p, :, HALO + h:HALO + NPAIR:2, IG * s:IG * s + IG].rearrange("p c m i -> p i c m")

        def bank_group(s, h):
            return p_in[s % 2][0:PAIR, IG * CR * h:IG * CR * (h + 1)].rearrange("p (i c m) -> p i c m", i=IG, c=CB)

        def rows_group(p, s):
            i = IG // 2 * s
            return ost[:, p, i:i + IG // 2, :].rearrange("p i (n r w) -> p (i n) r w", r=2, w=W)

        def bodies(eng, body, peeled=1):
            for it in range(peeled):
                body(it, it == 0, False)
            with eng.Fori(peeled, NBODY - 1) as it:
                body(it, False, False)
            body(NBODY - 1, False, True)

        def steps(eng, step):
            step(0, 0)
            step(1, 1)
            step(2, 0)
            with eng.Fori(1, (NIMG - 2) // 2) as q:
                step(2 * q + 1, 1)
                step(2 * q + 2, 0)
            step(NIMG - 1, 1)
            step(NIMG, 0)

        x_v = x.rearrange("b c h w -> b c (h w)")
        y_v = y_dram.ap().rearrange("b c h w -> b c (h w)")
        z_v = z_dram.ap().rearrange("b c h w -> b c (h w)")
        out_v = out.rearrange("b c h w -> b c (h w)")
        NSMALL = 12

        block = ctx.enter_context(nc.Block())

        @block.sync
        def _(sp):
            for dst, src in ((wa, dw_w.rearrange("c o h w -> c (o h w)")),
                             (wc, cw.rearrange("c o h w -> c (o h w)")),
                             (bias_a[:, :], dw_b.rearrange("(o c) -> o c", o=1).to_broadcast([TW, C])),
                             (bq[0], cb.rearrange("(o c) -> o c", o=1).to_broadcast([TW, C])),
                             (w1r[0:C], w1),
                             (w1r[C:C + 1], b1.rearrange("(o n) -> o n", o=1)),
                             (w2r[:, :, :], w2.rearrange("(t p) c -> p t c", p=128)),
                             (gam[:, :], grn_gamma.rearrange("(t p) -> p t", p=128)),
                             (bet[:, :], grn_beta.rearrange("(t p) -> p t", p=128)),
                             (lnw[:, :], ln_w.rearrange("(p o) -> p o", o=1)),
                             (lnb[:, :], ln_b.rearrange("(p o) -> p o", o=1)),
                             (b2c[:, :], b2.rearrange("(p o) -> p o", o=1))):
                sp.dma_start(dst, src, allow_slow_non_contiguous=True).then_inc(small_in, 16)
            sp.wait_ge(lines_made, 1)
            for n, (lines, made, kt) in enumerate(((lines_a[0], la_h, 4), (lines_a[1], la_l, 4), (lines_c[0], lc, 2))):
                sp.wait_ge(lines_made, 1 + n // 2)
                end = LPAD + C * TW * kt
                sp.dma_start(lines.ap()[LPAD:end].rearrange("(c n) -> c n", c=C), made).then_inc(lines_out, 16)
                sp.dma_start(lines.ap()[0:LPAD].rearrange("(o n) -> o n", o=1), zrow[:, 0:LPAD]).then_inc(lines_out, 16)
                sp.dma_start(lines.ap()[end:end + TW + LPAD].rearrange("(o n) -> o n", o=1), zrow).then_inc(lines_out, 16)
            sp.wait_ge(lines_out, 9 * 16)

            def conv_transfers(S, src, dst, lines, kt):
                rows_of, runs_of = (v.rearrange("(i g) c (m t) -> g (c m) i t", g=2, t=RUN) for v in (src, dst))

                def store(b, s):
                    sp.wait_ge(S["out"], G * b + G)
                    for g in range(2):
                        sp.dma_start(runs_of[g][bass.ds(b * CR, CR)], ost[CR * g:CR * g + CR, s, :, :]).then_inc(S[f"st{s}"], 16)

                def body(it, first, last):
                    for s in range(2):
                        b = 2 * it + s
                        need(sp, S["tin"], G * (b - 1))
                        for g in range(2):
                            sp.dma_start(xin[CR * g:CR * g + CR, s, :, :], rows_of[g][bass.ds(b * CR, CR)]).then_inc(S[f"x{s}"], 16)
                        need(sp, S["conv"], CB * (b - 1))
                        for part, buf in zip(lines, (toep_h, toep_l)):
                          for r in range(2):
                            rows = bass.AP(tensor=part, offset=b * (CB * kt * TW) + LPAD + r * LSTEP - (LSTEP - 1),
                                           ap=[[1, W], [TW, CB * kt], [1, TW]])
                            sp.dma_start(buf[W * r:W * r + W, s, :, 0:kt, :].bitcast(F32), rows).then_inc(S[f"t{s}"], 16)
                        if not (isinstance(b, int) and b < 3):
                            store(b - 3, 1 - s)
                bodies(sp, body, 2)
                for b in range(NBATCH - 3, NBATCH):
                    store(b, b % 2)

            sp.wait_ge(halo, 1)
            conv_transfers(stages["a"], x_v, y_v, lines_a, 4)

            for s in range(2):
                sp.wait_ge(stages["a"][f"st{s}"], 32 * NBODY)
            sp.wait_ge(stat_split, 1)
            for q in range(6):
                sp.dma_start(st_dram.ap()[q].rearrange("(g i) (m t) -> (i m) g t", i=IG, t=PAIR),
                             stb[:, q, :].rearrange("p (g t) -> p g t", g=G)).then_inc(stat_out, 16)
            sp.wait_ge(stat_out, 6 * 16)

            def load_y(i, p):
                need(sp, scale_done, NCH * (i - 1))
                sp.dma_start(yraw[:, p, :], y_v[i]).then_inc(y_in[p], 16)
                sp.dma_start(rows[:, p, :], st_dram.ap().rearrange("q i t -> i q t")[i]).then_inc(r_in[p], 16)

            def load_x(i, t):
                need(sp, v_ready, NCH * (i - 1) + t + 1)
                sp.dma_start(xr[:, CH * t:CH * t + CH], x_v[i][:, CH * t:CH * t + CH]).then_inc(x_in[t], 16)

            def store_z(i, p, t):
                sp.wait_ge(z_ready, NCH * i + t + 1)
                sp.dma_start(z_v[i][:, CH * t:CH * t + CH], zt[:, z_slot(p, t), :]).then_inc(z_out[z_slot(p, t)], 16)

            def step(i, p, more_y=True, more_x=True):
                if more_y:
                    load_y(i + 2, p)
                for t in range(NCH):
                    store_z(i - 1, 1 - p, t)
                    if more_x:
                        load_x(i, t)

            load_y(0, 0)
            load_y(1, 1)
            for t in range(NCH):
                load_x(0, t)
            load_y(2, 0)
            step(1, 1)
            step(2, 0)
            with sp.Fori(1, (NIMG - 4) // 2) as q:
                step(2 * q + 1, 1)
                step(2 * q + 2, 0)
            step(NIMG - 3, 1)
            step(NIMG - 2, 0, more_y=False)
            step(NIMG - 1, 1, more_y=False)
            step(NIMG, 0, more_y=False, more_x=False)
            for k in range(4):
                sp.wait_ge(z_out[k], 16 * Z_USES[k % 2] * NIMG // 2)
            sp.wait_ge(halo, 2)
            conv_transfers(stages["c"], z_v, out_v, lines_c, 2)
            for s in range(2):
                sp.wait_ge(stages["c"][f"st{s}"], 32 * NBODY)

        @block.gpsimd
        def _(pool):
            pool.memset(ident[:, :], 0.0).then_inc(prep, 1)
            pool.iota(rk[:, :].bitcast(I32), pattern=[[1, C]], base=1, channel_multiplier=0).then_inc(prep, 1)
            pool.memset(ones[:, :], 1.0).then_inc(consts, 1)
            pool.memset(pick_m[:, :], 0.0).then_inc(prep, 1)
            pool.memset(pick_r[:, :], 1.0).then_inc(prep, 1)
            pool.memset(halves[:, :], 0.5).then_inc(consts, 1)
            pool.wait_ge(prep, 4)
            pool.memset(pick_m[0:3, :], 1.0).then_inc(consts, 1)
            pool.memset(pick_r[0:3, :], 0.0).then_inc(consts, 1)
            pool.affine_select(out=ident[:, :], in_=ident[:, :], compare_op=ALU.not_equal, fill=1.0,
                               base=0, pattern=[[-1, 128]], channel_multiplier=1).then_inc(consts, 1)

            pool.wait_ge(halo, 1)

            def add(it, first, last):
                for k in range(2 * CB):
                    n = 2 * CB * it + k
                    pool.wait_ge(wel, 3 * n + 3)
                    need(pool, m2_done, n)
                    pool.tensor_tensor(m2, m2, dsq[:, k % 2, :], ALU.add).then_inc(m2_done, 1)
            bodies(pool, add)

            def low(i, p, t):
                n = NCH * i + t
                pool.wait_ge(yh_ready, n + 1)
                need(pool, h_done, MT * (n + 1 - NCH))
                pool.tensor_tensor(yl[0:C, CH * t:CH * t + CH], ct[:, 1 + (t + p) % 2, :], yh[0:C, CH * t:CH * t + CH].bitcast(F32),
                                   ALU.subtract).then_inc(yn_ready, 1)

            def step(i, p):
                fixed = isinstance(i, int)
                for t in range(NCH):
                    if t == NCH - 1 and not (fixed and i == NIMG):
                        pool.wait_ge(ss_ready, i + 1)
                        pool.tensor_tensor(gx[:, :], ss3[:, :], halves[:, :], ALU.pow).then_inc(gx_ready, 1)
                    if not (fixed and i >= NIMG - 1):
                        low(i + 1, 1 - p, t)

            for t in range(NCH):
                low(0, 0, t)
            steps(pool, step)

        @block.tensor
        def _(pe):
            pe.wait_ge(consts, 5)
            pe.wait_ge(small_in, 16 * NSMALL)
            pe.wait_ge(w1_made, 1)
            nc.tensor.matmul(bank[6][0:C + 1, 0:HID], lnb_last, w1r[0:C], start=True, stop=True)
            for t in range(MT):
                mm = nc.tensor.matmul(bank[7][0:C, 0:1], w2r[:, t, :], bet[:, t:t + 1], start=(t == 0), stop=(t == MT - 1))
            mm.then_inc(b1_mm, 1)

            def conv_stage(S, kt, slot0, parts):
                def tin(b, s, p):
                    n = G * b + s
                    if s == 0:
                        pe.wait_ge(S[f"x{p}"], 16 * (b - p) + 32)
                    need(pe, S["xt"], n - 1)
                    for h in range(2):
                        for i in range(IG // 2):
                            at = CM * (IG // 2 * h + i)
                            mm = nc.tensor.transpose(p_in[s % 2][0:PAIR, at:at + CM],
                                                     xin[:, p, IG // 2 * s + i, PAIR * h:PAIR * h + PAIR], ident[0:CM, 0:CM])
                    mm.then_inc(S["tin"], 1)

                def convolve(b, s, p, then_back):
                    n = CB * b + s
                    if s == 0:
                        loads = 32 * (2 if toep_l in [w for w, _ in parts] else 1)
                        pe.wait_ge(S[f"t{p}"], loads // 2 * (b - p) + loads)
                        pe.wait_ge(S["xt"], G * b + G)
                    need(pe, S["yt"], n - 1)
                    todo = [(k, w, v) for k in range(kt) for w, v in parts]
                    for n, (k, w, v) in enumerate(todo):
                        if then_back and n == len(todo) - 1:
                            back_waits(b - 1, s)
                        mm = nc.tensor.matmul(p_conv[s % 2][:, 0:NCOL], w[:, p, s, k, :],
                                              v[:, p, s, slot0 + k:slot0 + k + JP, :].rearrange("p j i -> p (j i)"),
                                              start=(n == 0), stop=(n == len(todo) - 1))
                    mm.then_inc(S["conv"], 1)

                def back_waits(b, s):
                    if s == 0:
                        pe.wait_ge(S["yt"], CB * b + CB)
                    need(pe, S["out"], G * b + s - 1)

                def back(b, s, p):
                    for n in range(IG):
                        i, h = divmod(n, 2)
                        i += IG // 2 * s
                        for r in range(2):
                            q = LSTEP * (1 - r)
                            mm = nc.tensor.transpose(p_back[s % 2][0:CM, 1 - r, LSTEP * n:LSTEP * n + LSTEP],
                                                     yt[q:q + LSTEP, p, i, (h + 1 - r) % 2].rearrange("p g m -> p (g m)"),
                                                     ident[q:q + LSTEP, q:q + LSTEP])
                    mm.then_inc(S["back"], 1)

                for s in range(G):
                    tin(0, s, 0)

                def body(it, first, last):
                    for p in range(2):
                        b = 2 * it + p
                        for s in range(G):
                            if not (last and p == 1):
                                tin(b + 1, s, 1 - p)
                            convolve(b, s, p, not (first and p == 0))
                            if not (first and p == 0):
                                back(b - 1, s, 1 - p)
                bodies(pe, body)
                for s in range(G):
                    back_waits(NBATCH - 1, s)
                    back(NBATCH - 1, s, 1)

            pe.wait_ge(b1_made, 2)
            conv_stage(stages["a"], 4, 0, ((toep_h, xt_h), (toep_h, xt_l), (toep_l, xt_h)))

            pe.wait_ge(stages["a"]["out"], C)
            pe.wait_ge(stat_in, 1)
            for q, v in enumerate((mean_in, rstd_in)):
                for g in range(G):
                    for r in range(2):
                        a = LSTEP * (1 - r)
                        mm = nc.tensor.transpose(p_stat[q][0:IG * NPAIR, 1 - r, LSTEP * g:LSTEP * g + LSTEP],
                                                 v[a:a + LSTEP, IG * NPAIR * g:IG * NPAIR * (g + 1)], ident[a:a + LSTEP, a:a + LSTEP])
            mm.then_inc(stat_t, 1)
            pe.wait_ge(stat_split, 1)

            def bcast(i, p, t):
                if t == 0:
                    pe.wait_ge(r_in[p], 8 * (i - p) + 16)
                need(pe, cen_done, NCH * i + t - 1)
                nc.tensor.matmul(p_mean[(t + p) % 2][0:C, 0:CH], pick_m[:, :], rows[:, p, CH * t:CH * t + CH], start=True, stop=True)
                need(pe, scale_done, NCH * i + t)
                nc.tensor.matmul(p_rstd[0:C, 0:CH], pick_r[:, :], rows[:, p, CH * t:CH * t + CH], start=True, stop=True).then_inc(bc_done, 1)

            def up(i, p, t):
                pe.wait_ge(yn_ready, NCH * i + t + 1)
                for m in range(MT):
                    need(pe, gelu_done, MT * (NCH * i + t) + m + 1 - MT)
                    w, cols = slice(128 * m, 128 * m + 128), slice(CH * t, CH * t + CH)
                    nc.tensor.matmul(p_h[m][:, 0:CH], w1h[:, w], yh[:, cols], start=True, stop=False)
                    nc.tensor.matmul(p_h[m][:, 0:CH], w1h[:, w], yl[:, cols], start=False, stop=False)
                    nc.tensor.matmul(p_h[m][:, 0:CH], w1l[:, w], yh[:, cols], start=False, stop=True).then_inc(h_done, 1)

            def down(i, p, t):
                if t == 0:
                    pe.wait_ge(w2_ready, i + 1)
                need(pe, v_ready, NCH * i + t - 1)
                k = (t + p) % 2
                for m in range(MT):
                    mm = nc.tensor.matmul(p_o[k][0:C, 0:CH], w2s[:, p, m, :], hid[:, p, m, CH * t:CH * t + CH],
                                          start=(m == 0), stop=(m == MT - 1))
                mm.then_inc(o_done, 1)

            def step(i, p):
                fixed = isinstance(i, int)
                head, tail = fixed and i == 0, fixed and i == NIMG
                ahead = not (fixed and i >= NIMG - 1)
                for t in range(NCH + LEAD):
                    if head and t < NCH - 1:
                        bcast(0, 0, t + 1)
                    if t < NCH and not tail:
                        up(i, p, t)
                    if t == 0 and not head:
                        pe.wait_ge(gx_ready, i)
                        need(pe, v_ready, NCH * (i - 1) - 1)
                        nc.tensor.matmul(p_grn[1 - p], ones[:, :], gx[:, :], start=True, stop=True).then_inc(gsum_done, 1)
                    if t >= LEAD and not head:
                        down(i - 1, 1 - p, t - LEAD)
                    if 0 <= t - BLEAD < NCH and ahead and not head:
                        bcast(i + 1, 1 - p, t - BLEAD)
                if head:
                    for t in range(NCH):
                        bcast(1, 1, t)
            pe.wait_ge(ones_row, 1)
            bcast(0, 0, 0)
            steps(pe, step)
            pe.wait_ge(v_ready, NCH * NIMG)
            conv_stage(stages["c"], 2, 1, ((toep_h, xt_h), (toep_h, xt_l)))

        @block.scalar
        def _(act):
            act.wait_ge(small_in, 16 * NSMALL)
            act.wait_ge(halo, 1)

            def conv_stage(S, bias, scale, rows_too):

                def xt_copy(b, s, p):
                    act.wait_ge(S["tin"], G * b + s + 1)
                    if s == 0:
                        need(act, S["conv"], CB * (b - 1))
                    for h in range(2):
                        ins = nc.scalar.activation(tile_group(xt_h, p, s, h), bank_group(s, h), ACT.Identity)
                    ins.then_inc(S["xh"], 1)

                def yt_copy(b, s, p):
                    n = CB * b + s
                    act.wait_ge(S["conv"], n + 1)
                    if s == 0:
                        need(act, S["back"], G * (b - 1))
                    if S is stages["a"]:
                        need(act, wel, 3 * (n - 2 * CB) + 1)
                    cols = p_conv[s % 2][:, 0:NCOL].rearrange("p (j i g) -> p i g j", i=NI2, g=2)
                    to = yt[:, p].rearrange("p i q g (c m) -> p q i g c m", c=CB)[:, :, :, :, s, :]
                    for part, q, shift in ((slice(0, TW), 1, 0), (slice(0, LSTEP), 0, 0), (slice(LSTEP, TW), 0, 1)):
                        j = q + 2 * shift
                        ins = nc.scalar.activation(to[part, q], cols[part, :, :, j:j + 2 * NRUN - 1:2], ACT.Identity,
                                                   bias=bias[part, bass.ds(n, 1)], scale=scale)
                    ins.then_inc(S["yt"], 1)

                def out_copy(b, s, p):
                    act.wait_ge(S["back"], G * b + s + 1)
                    if s == 0:
                        need(act, S[f"st{p}"], 16 * (b - p))
                    nc.scalar.activation(rows_group(p, s), forwards(p_back[s % 2][0:CM], IG), ACT.Identity).then_inc(S["out"], 1)

                for s in range(G):
                    xt_copy(0, s, 0)

                def body(it, first, last):
                    for p in range(2):
                        b = 2 * it + p
                        for s in range(G):
                            if not (last and p == 1):
                                xt_copy(b + 1, s, 1 - p)
                            yt_copy(b, s, p)
                            if rows_too and not (first and p == 0):
                                out_copy(b - 1, s, 1 - p)
                bodies(act, body)
                if rows_too:
                    for s in range(G):
                        out_copy(NBATCH - 1, s, 1)

            conv_stage(stages["a"], bias_a, 1.0, True)

            def squares(i, p, m, part):
                t0, t1 = ((0, SQ_SPLIT), (SQ_SPLIT, NCH))[part]
                act.wait_ge(gelu_done, MT * (NCH * i + t1 - 1) + m + 1)
                need(act, sq_act, 2 * MT * i + MT * part + m)
                nc.scalar.activation(sqd[:, 0:CH * (t1 - t0)], hid[:, p, m, CH * t0:CH * t1], ACT.Square,
                                     accum_out=ss[:, p, m, part:part + 1]).then_inc(sq_act, 1)

            act.wait_ge(var_ready, 1)
            nc.scalar.activation(root, var, ACT.Sqrt).then_inc(root_ready, 1)

            def step(i, p):
                fixed = isinstance(i, int)
                head, tail = fixed and i == 0, fixed and i == NIMG
                for t in range(NCH + LEAD):
                    if t < NCH and not tail:
                        if t == 0:
                            need(act, o_done, NCH * (i - 1))
                        for m in range(MT):
                            n = MT * (NCH * i + t) + m
                            act.wait_ge(h_done, n + 1)
                            nc.scalar.activation(hid[:, p, m, CH * t:CH * t + CH], p_h[m][:, 0:CH], ACT.Gelu).then_inc(gelu_done, 1)
                        if SQ_SPLIT <= t:
                            squares(i, p, t - SQ_SPLIT, 0)
                        if t == NCH - 1:
                            for m in range(MT):
                                squares(i, p, m, 1)
            steps(act, step)
            act.wait_ge(halo, 2)
            conv_stage(stages["c"], bias_c, -1.0 / FIX, False)

        @block.vector
        def _(dve):
            chain_sem = prep_step
            chain = [0]

            def link(ins):
                chain[0] += 1
                ins.then_inc(chain_sem, 1)
                dve.wait_ge(chain_sem, chain[0])

            def clear_halos():
                dve.memset(xt_h.rearrange("p a b c d -> p (a b c d)").bitcast(F32), 0.0)
                return dve.memset(xt_l.rearrange("p a b c d -> p (a b c d)").bitcast(F32), 0.0)

            link(clear_halos())
            dve.memset(mean, 0.0)
            dve.memset(m2, 0.0)
            dve.memset(la, 0.0)
            dve.memset(zrow, 0.0)
            link(dve.memset(lc, 0.0))
            dve.sem_inc(halo, 1)
            dve.wait_ge(prep, 2)
            link(dve.tensor_copy(ck[:, :], rk[:, :].bitcast(I32)))
            link(dve.reciprocal(rk[:, :], ck[:, :]))
            link(dve.tensor_scalar(ck[:, :], rk[:, :], -1.0, 1.0, ALU.mult, ALU.add))
            dve.wait_ge(small_in, 16 * NSMALL)
            for dy in range(7):
                for dx in range(7):
                    at = (dy + 1) * LSTEP + dx - 3
                    ins = dve.tensor_copy(la[:, at:at + 1], wa[:, 7 * dy + dx:7 * dy + dx + 1])
            link(ins)
            link(dve.tensor_copy(la_h.bitcast(F32R), la))
            link(dve.tensor_tensor(la_l.bitcast(F32R), la, la_h, ALU.subtract))
            dve.sem_inc(lines_made, 1)
            link(dve.tensor_scalar(wc1.bitcast(U32), wc.bitcast(U32), 0x7FFFFFFF, None, ALU.bitwise_and))
            link(dve.tensor_scalar(wc1, wc1, 2.0 ** -14, 1.0, ALU.max, ALU.min))
            link(dve.tensor_scalar(wc2.bitcast(U32), wc.bitcast(U32), 0x80000000, None, ALU.bitwise_and))
            link(dve.tensor_tensor(wc1.bitcast(U32), wc1.bitcast(U32), wc2.bitcast(U32), ALU.bitwise_or))
            link(dve.tensor_scalar(wc2, wc, 0.0, None, ALU.not_equal))
            link(dve.tensor_tensor(wc1, wc1, wc2, ALU.mult))
            link(dve.tensor_tensor(wc1, wc1, wc, ALU.subtract))
            link(dve.tensor_tensor(wc1, wc1, wc, ALU.add))
            link(dve.tensor_scalar(wc2, wc1, float(np.sqrt(2.0)), None, ALU.mult))
            link(dve.tensor_scalar(wc3.bitcast(U32), wc2.bitcast(U32), 0xFF800000, None, ALU.bitwise_and))
            link(dve.tensor_tensor(wc3, wc3, wc1, ALU.subtract))
            link(dve.tensor_tensor(wc3, wc3, wc1, ALU.add))
            for dy in range(3):
                for dx in range(3):
                    at = (dy + 1) * LSTEP + dx - 1
                    ins = dve.tensor_copy(lc[:, at:at + 1], wc3[:, 3 * dy + dx:3 * dy + dx + 1])
            link(ins)
            dve.sem_inc(lines_made, 1)
            link(dve.tensor_scalar(bq[1], bq[0], FIX, FIX * 32767.0, ALU.mult, ALU.min))
            link(dve.tensor_scalar(bq[1], bq[1], -FIX * 32768.0, None, ALU.max))
            link(dve.tensor_copy(bq[2].bitcast(I32), bq[1]))
            link(dve.tensor_tensor(bq[1], bq[1], bq[2].bitcast(I32), ALU.subtract))
            link(dve.scalar_tensor_tensor(out=bq[1], in0=bq[1], scalar=0.0, in1=bq[2].bitcast(I32), op0=ALU.is_lt, op1=ALU.subtract))
            link(dve.scalar_tensor_tensor(out=bq[1], in0=bq[1], scalar=-1.0 / FIX, in1=bq[0], op0=ALU.mult, op1=ALU.subtract))
            link(dve.tensor_tensor(bias_c[:, :], bq[1], bq[0], ALU.add))
            dve.memset(lnb_last, 0.0)
            link(dve.tensor_scalar(w1g[0:C], w1r[0:C], lnw[:, 0:1], None, ALU.mult))
            dve.tensor_copy(lnb_last[:, C:C + 1], lnb[:, :]).then_inc(w1_made, 1)
            dve.wait_ge(b1_mm, 1)
            link(dve.tensor_tensor(w1g[C:C + 1], bank[6][C:C + 1, 0:HID], w1r[C:C + 1], ALU.add))
            link(dve.tensor_copy(w1h[:, :], w1g))
            dve.tensor_tensor(w1l[:, :], w1g, w1h[:, :].bitcast(F32), ALU.subtract).then_inc(b1_made, 1)
            link(dve.tensor_tensor(cvec[:, :], bank[7][0:C, 0:1], b2c[:, :], ALU.add))
            dve.tensor_scalar(cvec[:, :], cvec[:, :], FIX, None, ALU.mult).then_inc(b1_made, 1)

            A = stages["a"]

            def runs(v):
                return v.rearrange("p (a m) -> p a m", m=NRUN)

            def low_part(S, b, s, p):
                n = G * b + s
                dve.wait_ge(S["xh"], n + 1)
                for h in range(2):
                    ins = dve.tensor_tensor(tile_group(xt_l, p, s, h), bank_group(s, h), tile_group(xt_h, p, s, h).bitcast(F32), ALU.subtract)
                ins.then_inc(S["xt"], 1)

            def conv_stage(S, update):
                for s in range(G):
                    low_part(S, 0, s, 0)

                def body(it, first, last):
                    for p in range(2):
                        b = 2 * it + p
                        for s in range(G):
                            if not (last and p == 1):
                                low_part(S, b + 1, s, 1 - p)
                            update(b, s, p)
                bodies(dve, body)

            def update(b, s, p):
                n = CB * b + s
                dve.wait_ge(A["yt"], n + 1)
                need(dve, wel, 3 * n)
                dve.tensor_tensor(runs(dev), yt[:, p].rearrange("p i q g (c m) -> p (i q g) c m", c=CB)[:, :, s], runs(mean), ALU.subtract).then_inc(wel, 1)
                dve.wait_ge(wel, 3 * n + 1)
                dve.scalar_tensor_tensor(out=mean, in0=dev, scalar=rk[:, bass.ds(n, 1)], in1=mean, op0=ALU.mult, op1=ALU.add).then_inc(wel, 1)
                need(dve, m2_done, n - 1)
                dve.scalar_tensor_tensor(out=dsq[:, s % 2, :], in0=dev, scalar=ck[:, bass.ds(n, 1)], in1=dev, op0=ALU.mult, op1=ALU.mult).then_inc(wel, 1)

            conv_stage(A, update)

            dve.wait_ge(wel, 3 * C)
            dve.wait_ge(m2_done, C)
            dve.tensor_scalar(var, m2, 1.0 / C, LN_EPS, ALU.mult, ALU.add).then_inc(var_ready, 1)

            def in_order(to, v):
                to = to.rearrange("p (i g m h) -> p h i g m", i=NI2, g=2, h=2)
                v = v.rearrange("p (i q g m) -> p q i g m", i=NI2, q=2, g=2)
                for second in range(2):
                    part = slice(LSTEP * second, LSTEP * second + LSTEP)
                    for h in range(2):
                        ins = dve.tensor_copy(to[part, h], v[part, (h + second) % 2])
                return ins
            in_order(mean_in, mean)
            dve.wait_ge(root_ready, 1)
            link(dve.reciprocal(rstd, root))
            link(dve.tensor_tensor(dsq[:, 0, :], rstd, rstd, ALU.mult))
            link(dve.tensor_tensor(dsq[:, 0, :], dsq[:, 0, :], var, ALU.mult))
            link(dve.tensor_scalar(dsq[:, 0, :], dsq[:, 0, :], -0.5, 1.5, ALU.mult, ALU.add))
            link(dve.tensor_tensor(rstd, rstd, dsq[:, 0, :], ALU.mult))
            in_order(rstd_in, rstd).then_inc(stat_in, 1)
            dve.wait_ge(stat_t, 1)
            for q in range(2):
                v = forwards(p_stat[q][0:IG * NPAIR], G)
                link(dve.tensor_copy(res1.rearrange("p (g h w) -> p g h w", g=G, h=2), v))
                link(dve.tensor_copy(stb[:, 3 * q, :], res1))
                link(dve.tensor_tensor(res2, res1, stb[:, 3 * q, :], ALU.subtract))
                link(dve.tensor_copy(stb[:, 3 * q + 1, :], res2))
                link(dve.tensor_tensor(res1, res2, stb[:, 3 * q + 1, :], ALU.subtract))
                link(dve.tensor_copy(stb[:, 3 * q + 2, :], res1))
            dve.sem_inc(stat_split, 1)

            def centre(i, p, t):
                dve.wait_ge(bc_done, NCH * i + t + 1)
                if t == 0:
                    dve.wait_ge(y_in[p], 8 * (i - p) + 16)
                dve.tensor_tensor(ct[:, 0, :], yraw[:, p, CH * t:CH * t + CH], p_mean[(t + p) % 2][0:C, 0:CH], ALU.subtract).then_inc(cen_done, 1)

            def scale(i, p, t):
                dve.wait_ge(cen_done, NCH * i + t + 1)
                need(dve, yn_ready, NCH * i + t - 1)
                dve.tensor_tensor(ct[:, 1 + (t + p) % 2, :], ct[:, 0, :], p_rstd[0:C, 0:CH], ALU.mult).then_inc(scale_done, 1)

            def high(i, p, t):
                dve.wait_ge(scale_done, NCH * i + t + 1)
                need(dve, h_done, MT * (NCH * (i - 1) + t + 1))
                dve.tensor_copy(yh[0:C, CH * t:CH * t + CH], ct[:, 1 + (t + p) % 2, :]).then_inc(yh_ready, 1)

            def normalise(i, p, t):
                for stage in (centre, scale, high):
                    stage(i, p, t)

            def grn_sums(i, p):
                dve.wait_ge(sq_act, 2 * MT * (i + 1))
                dve.tensor_reduce(ss3[:, :], ss[:, p, :, :], AX.X, ALU.add).then_inc(ss_ready, 1)

            def grn_scale(i, p):
                n = 5 * i
                dve.wait_ge(gsum_done, i + 1)
                dve.tensor_reduce(gsum[:, :], p_grn[p], AX.X, ALU.add).then_inc(grn_step, 1)
                dve.wait_ge(grn_step, n + 1)
                dve.tensor_scalar(gden[:, :], gsum[:, :], 1.0 / HID, GRN_EPS, ALU.mult, ALU.add).then_inc(grn_step, 1)
                dve.wait_ge(grn_step, n + 2)
                dve.reciprocal(grec[:, :], gden[:, :]).then_inc(grn_step, 1)
                dve.wait_ge(grn_step, n + 3)
                dve.scalar_tensor_tensor(out=gnx[:, :], in0=gx[:, :], scalar=grec[:, 0:1], in1=gam[:, :], op0=ALU.mult, op1=ALU.mult).then_inc(grn_step, 1)
                dve.wait_ge(grn_step, n + 4)
                dve.tensor_scalar(gsc[:, :], gnx[:, :], FIX, FIX, ALU.mult, ALU.add).then_inc(grn_step, 1)
                dve.wait_ge(grn_step, n + 5)
                for m in range(MT):
                    ins = dve.tensor_scalar(w2s[:, p, m, :], w2r[:, m, :], gsc[:, m:m + 1], None, ALU.mult)
                ins.then_inc(w2_ready, 1)

            def residual(i, p, t):
                n = NCH * i + t
                dve.wait_ge(o_done, n + 1)
                dve.wait_ge(x_in[t], 16 * i + 16)
                dve.scalar_tensor_tensor(out=vt[:, (t + p) % 2, :], in0=xr[:, CH * t:CH * t + CH], scalar=FIX,
                                         in1=p_o[(t + p) % 2][0:C, 0:CH], op0=ALU.mult, op1=ALU.add).then_inc(v_ready, 1)

            def nearest(i, p, t):
                k = (t + p) % 2
                dve.wait_ge(v_ready, NCH * i + t + 1)
                dve.tensor_scalar(rt[:, k, :], vt[:, k, :], cvec[:, 0:1], FIX * 32767.0, ALU.add, ALU.min).then_inc(r_ready, 1)

            def above(i, p, t):
                k = (t + p) % 2
                dve.wait_ge(r_ready, NCH * i + t + 1)
                dve.scalar_tensor_tensor(out=dt_[:, k, :], in0=vt[:, k, :], scalar=cvec[:, 0:1], in1=rt[:, k, :],
                                         op0=ALU.add, op1=ALU.subtract).then_inc(d_ready, 1)

            def floor_of(i, p, t):
                k = (t + p) % 2
                dve.wait_ge(d_ready, NCH * i + t + 1)
                need(dve, z_out[z_slot(p, t)], 8 * Z_USES[t % 2] * (i - p) + 16 * (t // 2))
                dve.scalar_tensor_tensor(out=zt[:, z_slot(p, t), :], in0=dt_[:, k, :], scalar=0.0, in1=rt[:, k, :],
                                         op0=ALU.is_lt, op1=ALU.subtract).then_inc(z_ready, 1)

            def step(i, p):
                fixed = isinstance(i, int)
                head, tail = fixed and i == 0, fixed and i == NIMG
                ahead = not (fixed and i >= NIMG - 1)
                if head:
                    for t in range(1, NCH):
                        normalise(0, 0, t)
                    for t in range(NCH):
                        if t == NCH - 1:
                            grn_sums(i, p)
                        normalise(1, 1, t)
                    return
                grn_scale(i - 1, 1 - p)
                if not (fixed and i == 1):
                    for stage in (residual, nearest, above, floor_of):
                        stage(i - 2, p, NCH - 1)
                for t in range(NCH):
                    if t == NCH - 1 and not tail:
                        grn_sums(i, p)
                    for norm, rnd in ((centre, residual), (scale, nearest), (high, above), (None, floor_of)):
                        if norm and ahead:
                            norm(i + 1, 1 - p, t)
                        if t > 0:
                            rnd(i - 1, 1 - p, t - 1)
                if tail:
                    for stage in (residual, nearest, above, floor_of):
                        stage(i - 1, 1 - p, NCH - 1)

            dve.memset(yh[C:C + 1, :].bitcast(F32), 1.0)
            dve.memset(yl[C:C + 1, :].bitcast(F32), 0.0).then_inc(ones_row, 1)
            normalise(0, 0, 0)
            steps(dve, step)
            dve.wait_ge(z_ready, NCH * NIMG)
            for k in range(4):
                dve.wait_ge(z_out[k], 16 * Z_USES[k % 2] * NIMG // 2)
            dve.wait_ge(sq_act, 2 * MT * NIMG)
            link(clear_halos())
            dve.sem_inc(halo, 1)
            S = stages["c"]

            def out_copy(b, s, p):
                dve.wait_ge(S["back"], G * b + s + 1)
                if s == 0:
                    need(dve, S[f"st{p}"], 16 * (b - p))
                dve.tensor_copy(rows_group(p, s), forwards(p_back[s % 2][0:CM], IG)).then_inc(S["out"], 1)

            def last_batch(b, s, p):
                if not (isinstance(b, int) and b == 0):
                    out_copy(b - 1, s, 1 - p)
            conv_stage(S, last_batch)
            for s in range(G):
                out_copy(NBATCH - 1, s, 1)


_INS = ["x", "L0_conv_dw_w", "L0_conv_dw_b", "L0_conv_ln_w", "L0_conv_ln_b", "L0_conv_w1", "L0_conv_b1",
        "L0_conv_grn_gamma", "L0_conv_grn_beta", "L0_conv_w2", "L0_conv_b2", "L1_conv_weight", "L1_conv_bias"]


def kernel(**inputs):
    import numpy as _np
    import concourse.bacc as _bacc
    from concourse import mybir as _mybir
    from concourse.bass_utils import run_bass_kernel_spmd as _run

    nc = _bacc.Bacc("TRN2", target_bir_lowering=False, num_devices=1)
    arrays, args = {}, []
    for name in _INS:
        a = _np.ascontiguousarray(inputs[name])
        arrays[f"in_{name}_dram"] = a
        args.append(nc.dram_tensor(f"in_{name}_dram", a.shape, _mybir.dt.from_np(a.dtype), kind="ExternalInput").ap())
    args.append(nc.dram_tensor("out_0_dram", (NIMG, C, H, W), F32, kind="ExternalOutput").ap())
    build(nc, *args)
    r = _run(nc, [arrays], core_ids=[0])
    return r.results[0]["out_0_dram"]
```

```python
from contextlib import ExitStack

import numpy as np

import concourse.bass as bass
from concourse import mybir

ALU = mybir.AluOpType
ACT = mybir.ActivationFunctionType
AX = mybir.AxisListType
F32 = mybir.dt.float32
F32R = mybir.dt.float32r
BF16 = mybir.dt.bfloat16
I32 = mybir.dt.int32
U32 = mybir.dt.uint32

NIMG, C, H, W = 16, 96, 56, 56
HID = 4 * C
HW = H * W
PAIR = 2 * W
NPAIR = H // 2
JP = NPAIR + 1
CB = 4
RUN = 4 * W
NRUN = H // 4
CR = CB * NRUN
CM = 2 * CR
NI2 = NIMG // 2
IG = 4
G = NIMG // IG
NBATCH = C // CB
NBODY = NBATCH // 2
HALO = 2
SLOTS = NPAIR + 2 * HALO
NPIX = NIMG * NPAIR
NCOL = NIMG * JP
LSTEP = 64
TW = 2 * LSTEP
LPAD = LSTEP
CH = 448
NCH = HW // CH
MT = HID // 128
FIX = 65536.0
AHEAD = ((0, 1), (2,), (3,), ())
LN_EPS = 1e-6
GRN_EPS = 1e-6
SQ_SPLIT = 4
SQ_WIDE = SQ_SPLIT * CH
Z_USES = ((NCH + 1) // 2, NCH // 2)
LEAD = 2
BLEAD = 1


def need(eng, sem, value):
    if isinstance(value, int) and value <= 0:
        return
    eng.wait_ge(sem, value)


def forwards(v, n):
    (part, (bank, _), (step, _)) = v.ap
    return bass.AP(tensor=v.tensor, offset=v.offset + LSTEP - 1,
                   ap=[part, [LSTEP, n], [bank, 2], [-1, W]])


def z_slot(p, t):
    return 2 * p + t % 2


def build(nc, x, dw_w, dw_b, ln_w, ln_b, w1, b1, grn_gamma, grn_beta, w2, b2, cw, cb, out):
    y_dram = nc.dram_tensor("y_scratch", (NIMG, C, H, W), F32)
    z_dram = nc.dram_tensor("z_scratch", (NIMG, C, H, W), F32)
    st_dram = nc.dram_tensor("stats_scratch", (6, NIMG, HW), BF16)
    KA, KC = 4, 2
    lines_a = nc.dram_tensor("lines_a", (LPAD + C * TW * KA + TW + LPAD,), F32)
    lines_c = nc.dram_tensor("lines_c", (LPAD + C * TW * KC + TW + LPAD,), F32)

    with ExitStack() as ctx:
        def sb(name, shape, dt=F32):
            return ctx.enter_context(nc.sbuf_tensor(name, shape, dt))

        def sem(name):
            return ctx.enter_context(nc.semaphore(name))

        ident = sb("ident", [128, 128])
        ones = sb("ones", [128, 128])
        pick_m = sb("pick_m", [6, C], BF16)
        pick_r = sb("pick_r", [6, C], BF16)
        halves = sb("halves", [128, MT])
        bias_a = sb("bias_a", [TW, C])
        bias_c = sb("bias_c", [TW, C])
        rk = sb("rk", [TW, C])
        ck = sb("ck", [TW, C])
        w1h = sb("w1h", [C + 1, HID], F32R)
        w1l = sb("w1l", [C + 1, HID], F32R)
        w2r = sb("w2r", [128, MT, C])
        w2s = sb("w2s", [128, 2, MT, C])
        gam = sb("gam", [128, MT])
        bet = sb("bet", [128, MT])
        lnw = sb("lnw", [C, 1])
        lnb = sb("lnb", [C, 1])
        b2c = sb("b2c", [C, 1])
        cvec = sb("cvec", [C, 1])
        ss = sb("ss", [128, 2, MT, 2])
        ss3 = sb("ss3", [128, MT])
        gx = sb("gx", [128, MT])
        gsum = sb("gsum", [128, 1])
        gden = sb("gden", [128, 1])
        grec = sb("grec", [128, 1])
        gnx = sb("gnx", [128, MT])
        gsc = sb("gsc", [128, MT])

        ARENA, ARENA_R = 28672, 16384
        arena = sb("arena", [128, ARENA])
        arena_r = sb("arena_r", [128, ARENA_R], F32R)

        class Carve:
            def __init__(self, region, limit):
                self.region, self.limit, self.at = region, limit, 0

            def __call__(self, parts, *dims):
                size = int(np.prod(dims))
                v = self.region[0:parts, self.at:self.at + size]
                self.at += size
                assert self.at <= self.limit, self.at
                if len(dims) > 1:
                    names = "abcdef"[:len(dims)]
                    v = v.rearrange(f"p ({' '.join(names)}) -> p {' '.join(names)}",
                                    **{n: d for n, d in zip(names[1:], dims[1:])})
                return v

        conv, conv_r = Carve(arena, ARENA), Carve(arena_r, ARENA_R)
        xin = conv(CM, 2, NI2, RUN)
        toep = conv(PAIR, 2, CB, KA * TW)
        toep_h = conv_r(PAIR, 2, CB, KA * TW)
        toep_l = conv_r(PAIR, 2, CB, KA * TW)
        xt_h = conv_r(PAIR, 2, CB, SLOTS, NIMG)
        xt_l = conv_r(PAIR, 2, CB, SLOTS, NIMG)
        yt = conv(TW, 2, NI2, 2, 2, CB * NRUN)
        ost = conv(CM, 2, NI2, RUN)
        mean = conv(TW, NPIX)
        m2 = conv(TW, NPIX)
        dev = conv(TW, NPIX)
        dsq = conv(TW, 2, NPIX)
        rstd = conv(TW, NPIX)
        var = conv(TW, NPIX)
        root = conv(TW, NPIX)
        mean_in = conv(TW, NPIX)
        rstd_in = conv(TW, NPIX)
        res1 = conv(IG * NPAIR, G * PAIR)
        res2 = conv(IG * NPAIR, G * PAIR)
        wa = conv(C, 49)
        wc = conv(C, 9)
        wc1 = conv(C, 9)
        wc2 = conv(C, 9)
        wc3 = conv(C, 9)
        la = conv(C, KA * TW)
        lc = conv(C, KC * TW)
        w1r = conv(C + 1, HID)
        w1g = conv(C + 1, HID)
        lnb_last = conv(C, C + 1)
        zrow = conv(1, TW + LPAD)
        bq = [conv(TW, C) for _ in range(3)]
        stb = conv(IG * NPAIR, 3 * G * PAIR).bitcast(BF16).rearrange("p (q n) -> p q n", q=6)

        mlp, mlp_r = Carve(arena, ARENA), Carve(arena_r, ARENA_R)
        yraw = mlp_r(C, 2, HW).bitcast(F32)
        rows = mlp_r(6, HW).bitcast(BF16).rearrange("q (s n) -> q s n", s=2)
        yh = mlp_r(C + 1, HW)
        yl = mlp_r(C + 1, HW)
        ct = mlp(C, 3, CH)
        xr = mlp(C, HW)
        hid = mlp(128, 2, MT, HW)
        vt = mlp(C, 2, CH)
        rt = mlp(C, 2, CH).bitcast(I32)
        dt = mlp(C, 2, CH)
        zt = mlp(C, 4, CH)
        sqd = mlp(128, SQ_WIDE // 2).bitcast(BF16)

        BANK = 512
        psum = ctx.enter_context(nc.psum_tensor("psum", [128, 8, BANK], F32))
        bank = [psum[:, i, :] for i in range(8)]
        p_in, p_conv = bank[0:2], bank[2:4]
        p_back = [psum[:, 4:6, :], psum[:, 6:8, :]]
        p_stat = [psum[:, 0:2, :], psum[:, 2:4, :]]
        p_h, p_mean, p_rstd, p_o = bank[0:3], bank[3:5], bank[5], bank[6:8]
        p_grn = [b[:, CH:CH + MT] for b in p_o]

        small_in = sem("small_in")
        dw_in = sem("dw_in")
        consts = sem("consts")
        prep = sem("prep")
        dve_chain = sem("dve_chain")
        halo = sem("halo")
        lines_made = sem("lines_made")
        lines_out = sem("lines_out")
        w1_made = sem("w1_made")
        b1_mm = sem("b1_mm")
        b1_made = sem("b1_made")
        stages = {k: {n: sem(f"{k}_{n}") for n in ("x0", "x1", "t0", "t1", "st0", "st1", "th", "tl", "tin", "xh", "xt",
                                                   "conv", "yt", "back", "out")} for k in "ac"}
        wel = sem("wel")
        m2_done = sem("m2_done")
        var_ready = sem("var_ready")
        root_ready = sem("root_ready")
        stat_in = sem("stat_in")
        stat_t = sem("stat_t")
        stat_split = sem("stat_split")
        stat_out = sem("stat_out")
        ones_row = sem("ones_row")
        y_in = [sem("y_in0"), sem("y_in1")]
        x_in = [sem(f"x_in{t}") for t in range(NCH)]
        r_in = [sem("r_in0"), sem("r_in1")]
        bc_done = sem("bc_done")
        cen_done = sem("cen_done")
        scale_done = sem("scale_done")
        yh_ready = sem("yh_ready")
        yn_ready = sem("yn_ready")
        xc_ready = sem("xc_ready")
        h_done = sem("h_done")
        gelu_done = sem("gelu_done")
        sq_act = sem("sq_act")
        ss_ready = sem("ss_ready")
        gx_ready = sem("gx_ready")
        gsum_done = sem("gsum_done")
        grn_step = sem("grn_step")
        w2_ready = sem("w2_ready")
        o_done = sem("o_done")
        v_ready = sem("v_ready")
        r_ready = sem("r_ready")
        d_ready = sem("d_ready")
        z_ready = sem("z_ready")
        z_out = [sem(f"z_out{i}") for i in range(4)]

        def tile_group(v, p, s, h):
            return v[:, p, :, HALO + h:HALO + NPAIR:2, IG * s:IG * s + IG].rearrange("p c m i -> p i c m")

        def bank_group(s, h):
            return p_in[s % 2][0:PAIR, IG * CR * h:IG * CR * (h + 1)].rearrange("p (i c m) -> p i c m", i=IG, c=CB)

        def rows_group(p, s):
            i = IG // 2 * s
            return ost[:, p, i:i + IG // 2, :].rearrange("p i (n r w) -> p (i n) r w", r=2, w=W)

        def bodies(eng, body, peeled=1):
            for it in range(peeled):
                body(it, it == 0, False)
            with eng.Fori(peeled, NBODY - 1) as it:
                body(it, False, False)
            body(NBODY - 1, False, True)

        def steps(eng, step):
            step(0, 0)
            step(1, 1)
            step(2, 0)
            with eng.Fori(1, (NIMG - 2) // 2) as q:
                step(2 * q + 1, 1)
                step(2 * q + 2, 0)
            step(NIMG - 1, 1)
            step(NIMG, 0)

        x_v = x.rearrange("b c h w -> b c (h w)")
        y_v = y_dram.ap().rearrange("b c h w -> b c (h w)")
        z_v = z_dram.ap().rearrange("b c h w -> b c (h w)")
        out_v = out.rearrange("b c h w -> b c (h w)")
        NSMALL = 11

        block = ctx.enter_context(nc.Block())

        @block.sync
        def _(sp):
            def load_rows(S, src, b, s):
                rows_of = src.rearrange("(i g) c (m t) -> g (c m) i t", g=2, t=RUN)
                for g in range(2):
                    sp.dma_start(xin[CR * g:CR * g + CR, s, :, :], rows_of[g][bass.ds(b * CR, CR)]).then_inc(S[f"x{s}"], 16)

            sp.dma_start(wa, dw_w.rearrange("c o h w -> c (o h w)")).then_inc(dw_in, 16)
            load_rows(stages["a"], x_v, 0, 0)
            for dst, src in ((wc, cw.rearrange("c o h w -> c (o h w)")),
                             (bias_a[:, :], dw_b.rearrange("(o c) -> o c", o=1).to_broadcast([TW, C])),
                             (bq[0], cb.rearrange("(o c) -> o c", o=1).to_broadcast([TW, C])),
                             (w1r[0:C], w1),
                             (w1r[C:C + 1], b1.rearrange("(o n) -> o n", o=1)),
                             (w2r[:, :, :], w2.rearrange("(t p) c -> p t c", p=128)),
                             (gam[:, :], grn_gamma.rearrange("(t p) -> p t", p=128)),
                             (bet[:, :], grn_beta.rearrange("(t p) -> p t", p=128)),
                             (lnw[:, :], ln_w.rearrange("(p o) -> p o", o=1)),
                             (lnb[:, :], ln_b.rearrange("(p o) -> p o", o=1)),
                             (b2c[:, :], b2.rearrange("(p o) -> p o", o=1))):
                sp.dma_start(dst, src, allow_slow_non_contiguous=True).then_inc(small_in, 16)

            def store_lines(lines, made, kt):
                end = LPAD + C * TW * kt
                sp.dma_start(lines.ap()[LPAD:end].rearrange("(c n) -> c n", c=C), made).then_inc(lines_out, 16)
                sp.dma_start(lines.ap()[0:LPAD].rearrange("(o n) -> o n", o=1), zrow[:, 0:LPAD]).then_inc(lines_out, 16)
                sp.dma_start(lines.ap()[end:end + TW + LPAD].rearrange("(o n) -> o n", o=1), zrow).then_inc(lines_out, 16)

            sp.wait_ge(lines_made, 1)
            store_lines(lines_a, la, KA)
            sp.wait_ge(lines_out, 3 * 16)

            def load_tables(S, lines, kt, buf, b, s):
                for r in range(2):
                    shifted = bass.AP(tensor=lines, offset=b * (CB * kt * TW) + LPAD + r * LSTEP - (LSTEP - 1),
                                      ap=[[1, W], [kt * TW, CB], [1, kt * TW]])
                    sp.dma_start(buf[W * r:W * r + W, s, :, 0:kt * TW], shifted).then_inc(S[f"t{s}"], 16)

            def tables_a(b, s):
                need(sp, stages["a"]["tl"], CB * (b - 1))
                load_tables(stages["a"], lines_a, KA, toep, b, s)

            def tables_c(b, s):
                need(sp, stages["c"]["conv"], CB * (b - 1))
                load_tables(stages["c"], lines_c, KC, toep_h.bitcast(F32), b, s)

            def conv_transfers(S, src, dst, tables, ahead):
                runs_of = dst.rearrange("(i g) c (m t) -> g (c m) i t", g=2, t=RUN)

                def store(b, s):
                    sp.wait_ge(S["out"], G * b + G)
                    for g in range(2):
                        sp.dma_start(runs_of[g][bass.ds(b * CR, CR)], ost[CR * g:CR * g + CR, s, :, :]).then_inc(S[f"st{s}"], 16)

                def body(it, first, last):
                    for s in range(2):
                        b = 2 * it + s
                        if not (last and s == 1):
                            need(sp, S["tin"], G * b)
                            load_rows(S, src, b + 1, 1 - s)
                            if ahead:
                                tables(b + 1, 1 - s)
                        if not ahead:
                            tables(b, s)
                        if not (isinstance(b, int) and b < 3):
                            store(b - 3, 1 - s)
                bodies(sp, body, 2)
                for b in range(NBATCH - 3, NBATCH):
                    store(b, b % 2)

            tables_a(0, 0)
            conv_transfers(stages["a"], x_v, y_v, tables_a, True)
            sp.wait_ge(lines_made, 2)
            store_lines(lines_c, lc, KC)

            for s in range(2):
                sp.wait_ge(stages["a"][f"st{s}"], 32 * NBODY)
            sp.wait_ge(lines_out, 6 * 16)

            def load_y(i, p):
                need(sp, cen_done, NCH * (i - 1))
                sp.dma_start(yraw[:, p, :], y_v[i]).then_inc(y_in[p], 16)

            def load_stats(i, p):
                need(sp, bc_done, NCH * (i - 1))
                sp.dma_start(rows[:, p, :], st_dram.ap().rearrange("q i t -> i q t")[i]).then_inc(r_in[p], 16)

            def load_x(i, t):
                need(sp, v_ready, NCH * (i - 1) + t + 1)
                sp.dma_start(xr[:, CH * t:CH * t + CH], x_v[i][:, CH * t:CH * t + CH]).then_inc(x_in[t], 16)

            def store_z(i, p, t):
                sp.wait_ge(z_ready, NCH * i + t + 1)
                sp.dma_start(z_v[i][:, CH * t:CH * t + CH], zt[:, z_slot(p, t), :]).then_inc(z_out[z_slot(p, t)], 16)

            def step(i, p, more_y=True, more_x=True):
                if more_y:
                    load_y(i + 2, p)
                    load_stats(i + 2, p)
                for t in range(NCH):
                    store_z(i - 1, 1 - p, t)
                    if more_x:
                        load_x(i, t)

            load_y(0, 0)
            load_y(1, 1)
            sp.wait_ge(wel, 3 * C)
            for t in range(NCH):
                load_x(0, t)
            for q in range(2):
                sp.wait_ge(stat_split, q + 1)
                sp.dma_start(st_dram.ap().rearrange("q (g i) (m t) -> (i m) (q g) t", i=IG, t=PAIR)[:, 3 * G * q:3 * G * (q + 1), :],
                             stb[:, 3 * q:3 * q + 3, :].rearrange("p q (g t) -> p (q g) t", g=G)).then_inc(stat_out, 16)
            sp.wait_ge(stat_out, 2 * 16)
            load_stats(0, 0)
            load_stats(1, 1)
            load_y(2, 0)
            load_stats(2, 0)
            step(1, 1)
            step(2, 0)
            with sp.Fori(1, (NIMG - 4) // 2) as q:
                step(2 * q + 1, 1)
                step(2 * q + 2, 0)
            step(NIMG - 3, 1)
            step(NIMG - 2, 0, more_y=False)
            step(NIMG - 1, 1, more_y=False)
            step(NIMG, 0, more_y=False, more_x=False)
            for k in range(4):
                sp.wait_ge(z_out[k], 16 * Z_USES[k % 2] * NIMG // 2)
            load_rows(stages["c"], z_v, 0, 0)
            sp.wait_ge(halo, 2)
            conv_transfers(stages["c"], z_v, out_v, tables_c, False)
            for s in range(2):
                sp.wait_ge(stages["c"][f"st{s}"], 32 * NBODY)

        @block.gpsimd
        def _(pool):
            pool.memset(ident[:, :], 0.0).then_inc(prep, 1)
            pool.iota(rk[:, :].bitcast(I32), pattern=[[1, C]], base=1, channel_multiplier=0).then_inc(prep, 1)
            pool.memset(ones[:, :], 1.0).then_inc(consts, 1)
            pool.memset(pick_m[:, :], 0.0).then_inc(prep, 1)
            pool.memset(pick_r[:, :], 1.0).then_inc(prep, 1)
            pool.memset(halves[:, :], 0.5).then_inc(consts, 1)
            pool.wait_ge(prep, 4)
            pool.memset(pick_m[0:3, :], 1.0).then_inc(consts, 1)
            pool.memset(pick_r[0:3, :], 0.0).then_inc(consts, 1)
            pool.affine_select(out=ident[:, :], in_=ident[:, :], compare_op=ALU.not_equal, fill=1.0,
                               base=0, pattern=[[-1, 128]], channel_multiplier=1).then_inc(consts, 1)

            A = stages["a"]
            pool.wait_ge(halo, 1)

            def table_low(b, s, p):
                pool.wait_ge(A["th"], CB * b + s + 1)
                need(pool, A["conv"], CB * (b - 2) + s + 1)
                pool.tensor_tensor(toep_l[:, p, s, :], toep[:, p, s, :], toep_h[:, p, s, :].bitcast(F32), ALU.subtract).then_inc(A["tl"], 1)

            for s in range(CB):
                table_low(0, s, 0)

            def add(it, first, last):
                for k in range(2 * CB):
                    p, s = divmod(k, CB)
                    b = 2 * it + p
                    n = CB * b + s
                    if not (last and p == 1):
                        for q in AHEAD[s]:
                            table_low(b + 1, q, 1 - p)
                    pool.wait_ge(wel, 3 * n + 3)
                    need(pool, m2_done, n)
                    pool.tensor_tensor(m2, m2, dsq[:, k % 2, :], ALU.add).then_inc(m2_done, 1)
            bodies(pool, add)

            pool.wait_ge(stages["a"]["conv"], C)
            pool.wait_ge(m2_done, C)
            pool.memset(yh[C:C + 1, :].bitcast(F32), 1.0).then_inc(ones_row, 1)
            pool.wait_ge(ones_row, 1)
            pool.memset(yl[C:C + 1, :].bitcast(F32), 0.0).then_inc(ones_row, 1)
            pool.wait_ge(ones_row, 2)

            def low(i, p, t):
                n = NCH * i + t
                pool.wait_ge(yh_ready, n + 1)
                need(pool, h_done, MT * (n + 1 - NCH))
                pool.tensor_tensor(yl[0:C, CH * t:CH * t + CH], ct[:, 1 + (t + p) % 2, :], yh[0:C, CH * t:CH * t + CH].bitcast(F32),
                                   ALU.subtract).then_inc(yn_ready, 1)

            def step(i, p):
                fixed = isinstance(i, int)
                for t in range(NCH):
                    if t == NCH - 1 and not (fixed and i == NIMG):
                        pool.wait_ge(ss_ready, i + 1)
                        pool.tensor_tensor(gx[:, :], ss3[:, :], halves[:, :], ALU.pow).then_inc(gx_ready, 1)
                    if not (fixed and i >= NIMG - 1):
                        low(i + 1, 1 - p, t)

            for t in range(NCH):
                low(0, 0, t)
            steps(pool, step)

        @block.tensor
        def _(pe):
            pe.wait_ge(consts, 5)

            def bias_products():
                pe.wait_ge(small_in, 16 * NSMALL)
                pe.wait_ge(w1_made, 1)
                nc.tensor.matmul(bank[6][0:C + 1, 0:HID], lnb_last, w1r[0:C], start=True, stop=True)
                for t in range(MT):
                    mm = nc.tensor.matmul(bank[7][0:C, 0:1], w2r[:, t, :], bet[:, t:t + 1], start=(t == 0), stop=(t == MT - 1))
                mm.then_inc(b1_mm, 1)

            def conv_stage(S, kt, slot0, parts, between=None):
                def tin(b, s, p):
                    n = G * b + s
                    if s == 0:
                        pe.wait_ge(S[f"x{p}"], 16 * (b - p) + 32)
                    need(pe, S["xt"], n - 1)
                    for h in range(2):
                        for i in range(IG // 2):
                            at = CM * (IG // 2 * h + i)
                            mm = nc.tensor.transpose(p_in[s % 2][0:PAIR, at:at + CM],
                                                     xin[:, p, IG // 2 * s + i, PAIR * h:PAIR * h + PAIR], ident[0:CM, 0:CM])
                    mm.then_inc(S["tin"], 1)

                def convolve(b, s, p, then_back):
                    n = CB * b + s
                    if s == 0:
                        if S is stages["a"]:
                            pe.wait_ge(S["tl"], CB * b + CB)
                        else:
                            pe.wait_ge(S[f"t{p}"], 16 * (b - p) + 32)
                        pe.wait_ge(S["xt"], G * b + G)
                    need(pe, S["yt"], n - 1)
                    todo = [(k, w, v) for k in range(kt) for w, v in parts]
                    for n, (k, w, v) in enumerate(todo):
                        if then_back and n == len(todo) - 1:
                            back_waits(b - 1, s)
                        mm = nc.tensor.matmul(p_conv[s % 2][:, 0:NCOL], w[:, p, s, TW * k:TW * k + TW],
                                              v[:, p, s, slot0 + k:slot0 + k + JP, :].rearrange("p j i -> p (j i)"),
                                              start=(n == 0), stop=(n == len(todo) - 1))
                    mm.then_inc(S["conv"], 1)

                def back_waits(b, s):
                    if s == 0:
                        pe.wait_ge(S["yt"], CB * b + CB)
                    need(pe, S["out"], G * b + s - 1)
                    if between and isinstance(b, int) and (b, s) == (0, 1):
                        pe.wait_ge(b1_made, 2)

                def back(b, s, p):
                    for n in range(IG):
                        i, h = divmod(n, 2)
                        i += IG // 2 * s
                        for r in range(2):
                            q = LSTEP * (1 - r)
                            mm = nc.tensor.transpose(p_back[s % 2][0:CM, 1 - r, LSTEP * n:LSTEP * n + LSTEP],
                                                     yt[q:q + LSTEP, p, i, (h + 1 - r) % 2].rearrange("p g m -> p (g m)"),
                                                     ident[q:q + LSTEP, q:q + LSTEP])
                    mm.then_inc(S["back"], 1)

                for s in range(G):
                    tin(0, s, 0)

                def body(it, first, last):
                    for p in range(2):
                        b = 2 * it + p
                        if between and first and p == 1:
                            between()
                        for s in range(G):
                            if not (last and p == 1):
                                for q in AHEAD[s]:
                                    tin(b + 1, q, 1 - p)
                            convolve(b, s, p, not (first and p == 0))
                            if not (first and p == 0):
                                back(b - 1, s, 1 - p)
                bodies(pe, body)
                for s in range(G):
                    back_waits(NBATCH - 1, s)
                    back(NBATCH - 1, s, 1)

            conv_stage(stages["a"], KA, 0, ((toep_h, xt_h), (toep_h, xt_l), (toep_l, xt_h)), bias_products)

            pe.wait_ge(stages["a"]["out"], C)
            for q, v in enumerate((mean_in, rstd_in)):
                pe.wait_ge(stat_in, q + 1)
                for g in range(G):
                    for r in range(2):
                        a = LSTEP * (1 - r)
                        mm = nc.tensor.transpose(p_stat[q][0:IG * NPAIR, 1 - r, LSTEP * g:LSTEP * g + LSTEP],
                                                 v[a:a + LSTEP, IG * NPAIR * g:IG * NPAIR * (g + 1)], ident[a:a + LSTEP, a:a + LSTEP])
                mm.then_inc(stat_t, 1)
            pe.wait_ge(stat_split, 2)

            def bcast(i, p, t):
                if t == 0:
                    pe.wait_ge(r_in[p], 8 * (i - p) + 16)
                need(pe, cen_done, NCH * i + t - 1)
                nc.tensor.matmul(p_mean[(t + p) % 2][0:C, 0:CH], pick_m[:, :], rows[:, p, CH * t:CH * t + CH], start=True, stop=True)
                need(pe, scale_done, NCH * i + t)
                nc.tensor.matmul(p_rstd[0:C, 0:CH], pick_r[:, :], rows[:, p, CH * t:CH * t + CH], start=True, stop=True).then_inc(bc_done, 1)

            def up(i, p, t):
                pe.wait_ge(yn_ready, NCH * i + t + 1)
                for m in range(MT):
                    need(pe, gelu_done, MT * (NCH * i + t) + m + 1 - MT)
                    w, cols = slice(128 * m, 128 * m + 128), slice(CH * t, CH * t + CH)
                    nc.tensor.matmul(p_h[m][:, 0:CH], w1h[:, w], yh[:, cols], start=True, stop=False)
                    nc.tensor.matmul(p_h[m][:, 0:CH], w1h[:, w], yl[:, cols], start=False, stop=False)
                    nc.tensor.matmul(p_h[m][:, 0:CH], w1l[:, w], yh[:, cols], start=False, stop=True).then_inc(h_done, 1)

            def down(i, p, t):
                if t == 0:
                    pe.wait_ge(w2_ready, i + 1)
                need(pe, v_ready, NCH * i + t - 1)
                k = (t + p) % 2
                for m in range(MT):
                    mm = nc.tensor.matmul(p_o[k][0:C, 0:CH], w2s[:, p, m, :], hid[:, p, m, CH * t:CH * t + CH],
                                          start=(m == 0), stop=(m == MT - 1))
                mm.then_inc(o_done, 1)

            def step(i, p):
                fixed = isinstance(i, int)
                head, tail = fixed and i == 0, fixed and i == NIMG
                ahead = not (fixed and i >= NIMG - 1)
                for t in range(NCH + LEAD):
                    if head and t < NCH - 1:
                        bcast(0, 0, t + 1)
                    if t < NCH and not tail:
                        up(i, p, t)
                    if t == 0 and not head:
                        pe.wait_ge(gx_ready, i)
                        need(pe, v_ready, NCH * (i - 1) - 1)
                        nc.tensor.matmul(p_grn[1 - p], ones[:, :], gx[:, :], start=True, stop=True).then_inc(gsum_done, 1)
                    if t >= LEAD and not head:
                        down(i - 1, 1 - p, t - LEAD)
                    if 0 <= t - BLEAD < NCH and ahead and not head:
                        bcast(i + 1, 1 - p, t - BLEAD)
                if head:
                    for t in range(NCH):
                        bcast(1, 1, t)

            pe.wait_ge(ones_row, 2)
            bcast(0, 0, 0)
            steps(pe, step)
            pe.wait_ge(v_ready, NCH * NIMG)
            conv_stage(stages["c"], KC, 1, ((toep_h, xt_h), (toep_h, xt_l)))

        @block.scalar
        def _(act):
            act.wait_ge(small_in, 16 * NSMALL)
            act.wait_ge(halo, 1)

            def conv_stage(S, bias, scale, rows_too):

                def xt_copy(b, s, p):
                    act.wait_ge(S["tin"], G * b + s + 1)
                    if s == 0:
                        need(act, S["conv"], CB * (b - 1))
                    for h in range(2):
                        ins = nc.scalar.activation(tile_group(xt_h, p, s, h), bank_group(s, h), ACT.Identity)
                    ins.then_inc(S["xh"], 1)

                def yt_copy(b, s, p):
                    n = CB * b + s
                    act.wait_ge(S["conv"], n + 1)
                    if s == 0:
                        need(act, S["back"], G * (b - 1))
                    if S is stages["a"]:
                        need(act, wel, 3 * (n - 2 * CB) + 1)
                    cols = p_conv[s % 2][:, 0:NCOL].rearrange("p (j i g) -> p i g j", i=NI2, g=2)
                    to = yt[:, p].rearrange("p i q g (c m) -> p q i g c m", c=CB)[:, :, :, :, s, :]
                    for part, q, shift in ((slice(0, TW), 1, 0), (slice(0, LSTEP), 0, 0), (slice(LSTEP, TW), 0, 1)):
                        j = q + 2 * shift
                        ins = nc.scalar.activation(to[part, q], cols[part, :, :, j:j + 2 * NRUN - 1:2], ACT.Identity,
                                                   bias=bias[part, bass.ds(n, 1)], scale=scale)
                    ins.then_inc(S["yt"], 1)

                def out_copy(b, s, p):
                    act.wait_ge(S["back"], G * b + s + 1)
                    if s == 0:
                        need(act, S[f"st{p}"], 16 * (b - p))
                    nc.scalar.activation(rows_group(p, s), forwards(p_back[s % 2][0:CM], IG), ACT.Identity).then_inc(S["out"], 1)

                def table_high(b, s, p):
                    if s == 0:
                        act.wait_ge(S[f"t{p}"], 16 * (b - p) + 32)
                    need(act, S["conv"], CB * (b - 2) + s + 1)
                    nc.scalar.activation(toep_h[:, p, s, :], toep[:, p, s, :], ACT.Identity).then_inc(S["th"], 1)

                for s in range(G):
                    xt_copy(0, s, 0)
                if rows_too:
                    for s in range(CB):
                        table_high(0, s, 0)

                def body(it, first, last):
                    for p in range(2):
                        b = 2 * it + p
                        for s in range(G):
                            if not (last and p == 1):
                                for q in AHEAD[s]:
                                    xt_copy(b + 1, q, 1 - p)
                                    if rows_too:
                                        table_high(b + 1, q, 1 - p)
                            yt_copy(b, s, p)
                            if rows_too and not (first and p == 0):
                                out_copy(b - 1, s, 1 - p)
                bodies(act, body)
                if rows_too:
                    for s in range(G):
                        out_copy(NBATCH - 1, s, 1)

            conv_stage(stages["a"], bias_a, 1.0, True)

            def squares(i, p, m, part):
                t0, t1 = ((0, SQ_SPLIT), (SQ_SPLIT, NCH))[part]
                act.wait_ge(gelu_done, MT * (NCH * i + t1 - 1) + m + 1)
                need(act, sq_act, 2 * MT * i + MT * part + m)
                nc.scalar.activation(sqd[:, 0:CH * (t1 - t0)], hid[:, p, m, CH * t0:CH * t1], ACT.Square,
                                     accum_out=ss[:, p, m, part:part + 1]).then_inc(sq_act, 1)

            def with_constant(i, t):
                cols = slice(CH * t, CH * t + CH)
                act.wait_ge(x_in[t], 16 * i + 16)
                nc.scalar.activation(xr[:, cols], xr[:, cols], ACT.Identity, bias=cvec[:, 0:1], scale=FIX).then_inc(xc_ready, 1)

            act.wait_ge(var_ready, 1)
            nc.scalar.activation(root, var, ACT.Sqrt).then_inc(root_ready, 1)

            def step(i, p):
                fixed = isinstance(i, int)
                tail = fixed and i == NIMG
                need(act, o_done, NCH * (i - 1))
                for t in range(NCH):
                    if not (fixed and i == 0):
                        with_constant(i - 1, t)
                    if tail:
                        continue
                    for m in range(MT):
                        n = MT * (NCH * i + t) + m
                        act.wait_ge(h_done, n + 1)
                        nc.scalar.activation(hid[:, p, m, CH * t:CH * t + CH], p_h[m][:, 0:CH], ACT.Gelu).then_inc(gelu_done, 1)
                    if SQ_SPLIT <= t:
                        squares(i, p, t - SQ_SPLIT, 0)
                if not tail:
                    for m in range(MT):
                        squares(i, p, m, 1)
            steps(act, step)
            act.wait_ge(halo, 2)
            conv_stage(stages["c"], bias_c, -1.0 / FIX, False)

        @block.vector
        def _(dve):
            chain = [0]

            def link(ins):
                chain[0] += 1
                ins.then_inc(dve_chain, 1)
                dve.wait_ge(dve_chain, chain[0])

            def clear_halos():
                for v in (xt_h, xt_l):
                    for slots in (slice(0, HALO), slice(HALO + NPAIR, SLOTS)):
                        ins = dve.memset(v[:, :, :, slots, :].bitcast(F32), 0.0)
                return ins

            link(clear_halos())
            dve.memset(mean, 0.0)
            dve.memset(m2, 0.0)
            dve.memset(la, 0.0)
            dve.memset(zrow, 0.0)
            link(dve.memset(lc, 0.0))
            dve.sem_inc(halo, 1)
            dve.wait_ge(prep, 2)
            link(dve.tensor_copy(ck[:, :], rk[:, :].bitcast(I32)))
            link(dve.reciprocal(rk[:, :], ck[:, :]))
            link(dve.tensor_scalar(ck[:, :], rk[:, :], -1.0, 1.0, ALU.mult, ALU.add))
            dve.wait_ge(dw_in, 16)
            for dy in range(7):
                for dx in range(7):
                    at = (dy + 1) * LSTEP + dx - 3
                    ins = dve.tensor_copy(la[:, at:at + 1], wa[:, 7 * dy + dx:7 * dy + dx + 1])
            link(ins)
            dve.sem_inc(lines_made, 1)

            def setup():
                dve.wait_ge(small_in, 16 * NSMALL)
                link(dve.tensor_scalar(wc1.bitcast(U32), wc.bitcast(U32), 0x7FFFFFFF, None, ALU.bitwise_and))
                link(dve.tensor_scalar(wc1, wc1, 2.0 ** -14, 1.0, ALU.max, ALU.min))
                link(dve.tensor_scalar(wc2.bitcast(U32), wc.bitcast(U32), 0x80000000, None, ALU.bitwise_and))
                link(dve.tensor_tensor(wc1.bitcast(U32), wc1.bitcast(U32), wc2.bitcast(U32), ALU.bitwise_or))
                link(dve.tensor_scalar(wc2, wc, 0.0, None, ALU.not_equal))
                link(dve.tensor_tensor(wc1, wc1, wc2, ALU.mult))
                link(dve.tensor_tensor(wc1, wc1, wc, ALU.subtract))
                link(dve.tensor_tensor(wc1, wc1, wc, ALU.add))
                link(dve.tensor_scalar(wc2, wc1, float(np.sqrt(2.0)), None, ALU.mult))
                link(dve.tensor_scalar(wc3.bitcast(U32), wc2.bitcast(U32), 0xFF800000, None, ALU.bitwise_and))
                link(dve.tensor_tensor(wc3, wc3, wc1, ALU.subtract))
                link(dve.tensor_tensor(wc3, wc3, wc1, ALU.add))
                for dy in range(3):
                    for dx in range(3):
                        at = (dy + 1) * LSTEP + dx - 1
                        ins = dve.tensor_copy(lc[:, at:at + 1], wc3[:, 3 * dy + dx:3 * dy + dx + 1])
                link(ins)
                dve.sem_inc(lines_made, 1)
                link(dve.tensor_scalar(bq[1], bq[0], FIX, FIX * 32767.0, ALU.mult, ALU.min))
                link(dve.tensor_scalar(bq[1], bq[1], -FIX * 32768.0, None, ALU.max))
                link(dve.tensor_copy(bq[2].bitcast(I32), bq[1]))
                link(dve.tensor_tensor(bq[1], bq[1], bq[2].bitcast(I32), ALU.subtract))
                link(dve.scalar_tensor_tensor(out=bq[1], in0=bq[1], scalar=0.0, in1=bq[2].bitcast(I32), op0=ALU.is_lt, op1=ALU.subtract))
                link(dve.scalar_tensor_tensor(out=bq[1], in0=bq[1], scalar=-1.0 / FIX, in1=bq[0], op0=ALU.mult, op1=ALU.subtract))
                link(dve.tensor_tensor(bias_c[:, :], bq[1], bq[0], ALU.add))
                dve.memset(lnb_last, 0.0)
                link(dve.tensor_scalar(w1g[0:C], w1r[0:C], lnw[:, 0:1], None, ALU.mult))
                dve.tensor_copy(lnb_last[:, C:C + 1], lnb[:, :]).then_inc(w1_made, 1)

            def finish_setup():
                dve.wait_ge(b1_mm, 1)
                link(dve.tensor_tensor(w1g[C:C + 1], bank[6][C:C + 1, 0:HID], w1r[C:C + 1], ALU.add))
                link(dve.tensor_copy(w1h[:, :], w1g))
                dve.tensor_tensor(w1l[:, :], w1g, w1h[:, :].bitcast(F32), ALU.subtract).then_inc(b1_made, 1)
                link(dve.tensor_tensor(cvec[:, :], bank[7][0:C, 0:1], b2c[:, :], ALU.add))
                dve.tensor_scalar(cvec[:, :], cvec[:, :], FIX, None, ALU.mult).then_inc(b1_made, 1)

            A = stages["a"]

            def runs(v):
                return v.rearrange("p (a m) -> p a m", m=NRUN)

            def low_part(S, b, s, p):
                n = G * b + s
                dve.wait_ge(S["xh"], n + 1)
                for h in range(2):
                    ins = dve.tensor_tensor(tile_group(xt_l, p, s, h), bank_group(s, h), tile_group(xt_h, p, s, h).bitcast(F32), ALU.subtract)
                ins.then_inc(S["xt"], 1)

            def conv_stage(S, update, first_thing=None, between=None):
                for s in range(G):
                    low_part(S, 0, s, 0)
                if first_thing:
                    first_thing()

                def body(it, first, last):
                    for p in range(2):
                        b = 2 * it + p
                        if between and first and p == 1:
                            between()
                        for s in range(G):
                            if not (last and p == 1):
                                for q in AHEAD[s]:
                                    low_part(S, b + 1, q, 1 - p)
                            update(b, s, p)
                bodies(dve, body)

            def update(b, s, p):
                n = CB * b + s
                dve.wait_ge(A["yt"], n + 1)
                need(dve, wel, 3 * n)
                dve.tensor_tensor(runs(dev), yt[:, p].rearrange("p i q g (c m) -> p (i q g) c m", c=CB)[:, :, s], runs(mean), ALU.subtract).then_inc(wel, 1)
                dve.wait_ge(wel, 3 * n + 1)
                dve.scalar_tensor_tensor(out=mean, in0=dev, scalar=rk[:, bass.ds(n, 1)], in1=mean, op0=ALU.mult, op1=ALU.add).then_inc(wel, 1)
                need(dve, m2_done, n - 1)
                dve.scalar_tensor_tensor(out=dsq[:, s % 2, :], in0=dev, scalar=ck[:, bass.ds(n, 1)], in1=dev, op0=ALU.mult, op1=ALU.mult).then_inc(wel, 1)

            conv_stage(A, update, setup, finish_setup)

            dve.wait_ge(wel, 3 * C)
            dve.wait_ge(m2_done, C)
            dve.tensor_scalar(var, m2, 1.0 / C, LN_EPS, ALU.mult, ALU.add).then_inc(var_ready, 1)

            def in_order(to, v):
                to = to.rearrange("p (i g m h) -> p h i g m", i=NI2, g=2, h=2)
                v = v.rearrange("p (i q g m) -> p q i g m", i=NI2, q=2, g=2)
                for second in range(2):
                    part = slice(LSTEP * second, LSTEP * second + LSTEP)
                    for h in range(2):
                        ins = dve.tensor_copy(to[part, h], v[part, (h + second) % 2])
                return ins
            in_order(mean_in, mean).then_inc(stat_in, 1)

            def split(q):
                dve.wait_ge(stat_t, q + 1)
                v = forwards(p_stat[q][0:IG * NPAIR], G)
                link(dve.tensor_copy(res1.rearrange("p (g h w) -> p g h w", g=G, h=2), v))
                link(dve.tensor_copy(stb[:, 3 * q, :], res1))
                link(dve.tensor_tensor(res2, res1, stb[:, 3 * q, :], ALU.subtract))
                link(dve.tensor_copy(stb[:, 3 * q + 1, :], res2))
                link(dve.tensor_tensor(res1, res2, stb[:, 3 * q + 1, :], ALU.subtract))
                link(dve.tensor_copy(stb[:, 3 * q + 2, :], res1))
                dve.sem_inc(stat_split, 1)

            split(0)
            dve.wait_ge(root_ready, 1)
            link(dve.reciprocal(rstd, root))
            link(dve.tensor_tensor(dsq[:, 0, :], rstd, rstd, ALU.mult))
            link(dve.tensor_tensor(dsq[:, 0, :], dsq[:, 0, :], var, ALU.mult))
            link(dve.tensor_scalar(dsq[:, 0, :], dsq[:, 0, :], -0.5, 1.5, ALU.mult, ALU.add))
            link(dve.tensor_tensor(rstd, rstd, dsq[:, 0, :], ALU.mult))
            in_order(rstd_in, rstd).then_inc(stat_in, 1)
            split(1)

            def centre(i, p, t):
                dve.wait_ge(bc_done, NCH * i + t + 1)
                if t == 0:
                    dve.wait_ge(y_in[p], 8 * (i - p) + 16)
                dve.tensor_tensor(ct[:, 0, :], yraw[:, p, CH * t:CH * t + CH], p_mean[(t + p) % 2][0:C, 0:CH], ALU.subtract).then_inc(cen_done, 1)

            def scale(i, p, t):
                dve.wait_ge(cen_done, NCH * i + t + 1)
                need(dve, yn_ready, NCH * i + t - 1)
                dve.tensor_tensor(ct[:, 1 + (t + p) % 2, :], ct[:, 0, :], p_rstd[0:C, 0:CH], ALU.mult).then_inc(scale_done, 1)

            def high(i, p, t):
                dve.wait_ge(scale_done, NCH * i + t + 1)
                need(dve, h_done, MT * (NCH * (i - 1) + t + 1))
                dve.tensor_copy(yh[0:C, CH * t:CH * t + CH], ct[:, 1 + (t + p) % 2, :]).then_inc(yh_ready, 1)

            def normalise(i, p, t):
                for stage in (centre, scale, high):
                    stage(i, p, t)

            def grn_sums(i, p):
                dve.wait_ge(sq_act, 2 * MT * (i + 1))
                dve.tensor_reduce(ss3[:, :], ss[:, p, :, :], AX.X, ALU.add).then_inc(ss_ready, 1)

            def grn_scale(i, p):
                n = 5 * i
                dve.wait_ge(gsum_done, i + 1)
                dve.tensor_reduce(gsum[:, :], p_grn[p], AX.X, ALU.add).then_inc(grn_step, 1)
                dve.wait_ge(grn_step, n + 1)
                dve.tensor_scalar(gden[:, :], gsum[:, :], 1.0 / HID, GRN_EPS, ALU.mult, ALU.add).then_inc(grn_step, 1)
                dve.wait_ge(grn_step, n + 2)
                dve.reciprocal(grec[:, :], gden[:, :]).then_inc(grn_step, 1)
                dve.wait_ge(grn_step, n + 3)
                dve.scalar_tensor_tensor(out=gnx[:, :], in0=gx[:, :], scalar=grec[:, 0:1], in1=gam[:, :], op0=ALU.mult, op1=ALU.mult).then_inc(grn_step, 1)
                dve.wait_ge(grn_step, n + 4)
                dve.tensor_scalar(gsc[:, :], gnx[:, :], FIX, FIX, ALU.mult, ALU.add).then_inc(grn_step, 1)
                dve.wait_ge(grn_step, n + 5)
                for m in range(MT):
                    ins = dve.tensor_scalar(w2s[:, p, m, :], w2r[:, m, :], gsc[:, m:m + 1], None, ALU.mult)
                ins.then_inc(w2_ready, 1)

            def residual(i, p, t):
                n = NCH * i + t
                dve.wait_ge(o_done, n + 1)
                dve.wait_ge(xc_ready, n + 1)
                dve.tensor_tensor(vt[:, (t + p) % 2, :], xr[:, CH * t:CH * t + CH], p_o[(t + p) % 2][0:C, 0:CH], ALU.add).then_inc(v_ready, 1)

            def nearest(i, p, t):
                k = (t + p) % 2
                dve.wait_ge(v_ready, NCH * i + t + 1)
                dve.tensor_scalar(rt[:, k, :], vt[:, k, :], -FIX * 32768.0, FIX * 32767.0, ALU.max, ALU.min).then_inc(r_ready, 1)

            def above(i, p, t):
                k = (t + p) % 2
                dve.wait_ge(r_ready, NCH * i + t + 1)
                dve.tensor_tensor(dt[:, k, :], vt[:, k, :], rt[:, k, :], ALU.subtract).then_inc(d_ready, 1)

            def floor_of(i, p, t):
                k = (t + p) % 2
                dve.wait_ge(d_ready, NCH * i + t + 1)
                need(dve, z_out[z_slot(p, t)], 8 * Z_USES[t % 2] * (i - p) + 16 * (t // 2))
                dve.scalar_tensor_tensor(out=zt[:, z_slot(p, t), :], in0=dt[:, k, :], scalar=0.0, in1=rt[:, k, :],
                                         op0=ALU.is_lt, op1=ALU.subtract).then_inc(z_ready, 1)

            def step(i, p):
                fixed = isinstance(i, int)
                head, tail = fixed and i == 0, fixed and i == NIMG
                ahead = not (fixed and i >= NIMG - 1)
                if head:
                    for t in range(1, NCH):
                        normalise(0, 0, t)
                    for t in range(NCH):
                        if t == NCH - 1:
                            grn_sums(i, p)
                        normalise(1, 1, t)
                    return
                grn_scale(i - 1, 1 - p)
                if not (fixed and i == 1):
                    for stage in (residual, nearest, above, floor_of):
                        stage(i - 2, p, NCH - 1)
                for t in range(NCH):
                    if t == NCH - 1 and not tail:
                        grn_sums(i, p)
                    for norm, rnd in ((centre, residual), (scale, nearest), (high, above), (None, floor_of)):
                        if norm and ahead:
                            norm(i + 1, 1 - p, t)
                        if t > 0:
                            rnd(i - 1, 1 - p, t - 1)
                if tail:
                    for stage in (residual, nearest, above, floor_of):
                        stage(i - 1, 1 - p, NCH - 1)

            normalise(0, 0, 0)
            steps(dve, step)
            dve.wait_ge(z_ready, NCH * NIMG)
            dve.wait_ge(sq_act, 2 * MT * NIMG)
            link(clear_halos())
            dve.sem_inc(halo, 1)
            S = stages["c"]

            def out_copy(b, s, p):
                dve.wait_ge(S["back"], G * b + s + 1)
                if s == 0:
                    need(dve, S[f"st{p}"], 16 * (b - p))
                dve.tensor_copy(rows_group(p, s), forwards(p_back[s % 2][0:CM], IG)).then_inc(S["out"], 1)

            def last_batch(b, s, p):
                if not (isinstance(b, int) and b == 0):
                    out_copy(b - 1, s, 1 - p)
            conv_stage(S, last_batch)
            for s in range(G):
                out_copy(NBATCH - 1, s, 1)


_INS = ["x", "L0_conv_dw_w", "L0_conv_dw_b", "L0_conv_ln_w", "L0_conv_ln_b", "L0_conv_w1", "L0_conv_b1",
        "L0_conv_grn_gamma", "L0_conv_grn_beta", "L0_conv_w2", "L0_conv_b2", "L1_conv_weight", "L1_conv_bias"]


def kernel(**inputs):
    import numpy as _np
    import concourse.bacc as _bacc
    from concourse import mybir as _mybir
    from concourse.bass_utils import run_bass_kernel_spmd as _run

    nc = _bacc.Bacc("TRN2", target_bir_lowering=False, num_devices=1)
    arrays, args = {}, []
    for name in _INS:
        a = _np.ascontiguousarray(inputs[name])
        arrays[f"in_{name}_dram"] = a
        args.append(nc.dram_tensor(f"in_{name}_dram", a.shape, _mybir.dt.from_np(a.dtype), kind="ExternalInput").ap())
    args.append(nc.dram_tensor("out_0_dram", (NIMG, C, H, W), F32, kind="ExternalOutput").ap())
    build(nc, *args)
    r = _run(nc, [arrays], core_ids=[0])
    return r.results[0]["out_0_dram"]
```
